# Optimizing a Trainium2 kernel written in Bass

```python
import numpy as np
import jax
import jax.numpy as jnp

def _softmax(x, axis=-1):
    return jax.nn.softmax(x, axis=axis)

def _gelu(x):
    return jax.nn.gelu(x, approximate=True)

def _silu(x):
    return jax.nn.silu(x)

def _sigmoid(x):
    return jax.nn.sigmoid(x)

def _layernorm(x, axis=-1, eps=1e-05):
    m = jnp.mean(x, axis=axis, keepdims=True)
    v = jnp.var(x, axis=axis, keepdims=True)
    return (x - m) / jnp.sqrt(v + eps)

def _scatter_add(tgt, idx, src, axis=0):
    return tgt.at[idx].add(src)

def _segment_sum(src, seg, n):
    return jax.ops.segment_sum(src, seg, n)
kernel_name = 'mk_vit_tower_postln_d1_tok_img768_r4_9e89ca'

def setup_inputs(seed: int=0):
    np.random.seed(seed)
    _w = jnp.asarray

    def _rec_inputs():
        import jax
        import jax.numpy as jnp
        _rk = jax.random.key(seed)
        x = -0.00040386 + 0.999972 * jax.random.normal(jax.random.fold_in(_rk, 1), (32, 64, 64, 3), jnp.float32)
        return x
    x = _rec_inputs()

    def _L0_tok_setup():
        import jax, jax.numpy as jnp
        import numpy as np
        IMG = 64
        PATCH = 16
        C = 3
        D = 192
        NP_ = (IMG // PATCH) ** 2
        B = 64

        def _patchify(x):
            Bn, H, Wd, Cn = x.shape
            hp, wp = (H // PATCH, Wd // PATCH)
            x = x.reshape(Bn, hp, PATCH, wp, PATCH, Cn)
            x = x.transpose(0, 1, 3, 2, 4, 5)
            return x.reshape(Bn, hp * wp, PATCH * PATCH * Cn)
        key = jax.random.key(seed)
        k1, k2, k3 = jax.random.split(key, 3)
        x = jax.random.normal(k1, (B, IMG, IMG, C), dtype=jnp.float32)
        patch_dim = C * PATCH * PATCH
        W = jax.random.normal(k2, (patch_dim, D), dtype=jnp.float32) / np.sqrt(patch_dim)
        b = jnp.zeros((D,), dtype=jnp.float32)
        pos_emb = jax.random.normal(k3, (NP_, D), dtype=jnp.float32) * 0.02
        return {'x': x, 'W': W, 'b': b, 'pos_emb': pos_emb}
    _L0_tok_all = _L0_tok_setup()
    _L0_tok_in = {k: v for k, v in _L0_tok_all.items() if k in ('W', 'b', 'pos_emb')}
    del _L0_tok_all

    def _L0_attn_setup():
        import jax, jax.numpy as jnp
        import numpy as np
        EMBED_DIM = 192
        NUM_HEADS = 12
        HEAD_DIM = EMBED_DIM // NUM_HEADS
        SEG_LEN = 64
        DILATION = 1

        def _dilated_mask(seq_len):
            idx = jnp.arange(seq_len)
            seg_id = idx // SEG_LEN
            on_stride = idx % SEG_LEN % DILATION == 0
            valid = (seg_id[:, None] == seg_id[None, :]) & on_stride[:, None] & on_stride[None, :]
            return jnp.where(valid, 0.0, -jnp.inf).astype(jnp.float32)
        key = jax.random.key(seed)
        ks = jax.random.split(key, 9)
        B, S, E = (2, 512, EMBED_DIM)
        w = lambda k: jax.random.normal(k, (E, E), jnp.float32) * 0.02
        b = lambda k: jax.random.normal(k, (E,), jnp.float32) * 0.02
        return {'x': jax.random.normal(ks[0], (B, S, E), jnp.float32), 'Wq': w(ks[1]), 'bq': b(ks[2]), 'Wk': w(ks[3]), 'bk': b(ks[4]), 'Wv': w(ks[5]), 'bv': b(ks[6]), 'Wo': w(ks[7]), 'bo': b(ks[8])}
    _L0_attn_all = _L0_attn_setup()
    _L0_attn_in = {k: v for k, v in _L0_attn_all.items() if k in ('Wq', 'bq', 'Wk', 'bk', 'Wv', 'bv', 'Wo', 'bo')}
    del _L0_attn_all

    def _L0_ffn_setup():
        import jax, jax.numpy as jnp
        import numpy as np
        DIM = 192
        NUM_HEADS = 12
        HEAD_DIM = DIM // NUM_HEADS
        SCALE = HEAD_DIM ** (-0.5)
        NUM_EXPERTS = 8
        RANK = 16
        ALPHA = 32
        TOPK = 2
        SCALING = ALPHA / RANK
        B, S = (8, 256)
        key = jax.random.key(seed)
        ks = jax.random.split(key, 12)
        d, e, r = (DIM, NUM_EXPERTS, RANK)
        inp = {'x': jax.random.normal(ks[0], (B, S, d), jnp.float32), 'Wg': jax.random.normal(ks[1], (e, d), jnp.float32) * 0.02, 'bg': jax.random.normal(ks[2], (e,), jnp.float32) * 0.02, 'Wqkv': jax.random.normal(ks[3], (3 * d, d), jnp.float32) * 0.02, 'bqkv': jax.random.normal(ks[4], (3 * d,), jnp.float32) * 0.02, 'Wproj': jax.random.normal(ks[5], (d, d), jnp.float32) * 0.02, 'bproj': jax.random.normal(ks[6], (d,), jnp.float32) * 0.02, 'A': jax.random.normal(ks[7], (e, r, d), jnp.float32) * 0.05, 'ba': jax.random.normal(ks[8], (e, r), jnp.float32) * 0.02, 'Bm': jax.random.normal(ks[9], (e, 3 * d, r), jnp.float32) * 0.05, 'bb': jax.random.normal(ks[10], (e, 3 * d), jnp.float32) * 0.02}
        return inp
    _L0_ffn_all = _L0_ffn_setup()
    _L0_ffn_in = {k: v for k, v in _L0_ffn_all.items() if k in ('Wg', 'bg', 'Wqkv', 'bqkv', 'Wproj', 'bproj', 'A', 'ba', 'Bm', 'bb')}
    del _L0_ffn_all
    return {'x': x, 'L0_tok_W': _L0_tok_in['W'], 'L0_tok_b': _L0_tok_in['b'], 'L0_tok_pos_emb': _L0_tok_in['pos_emb'], 'L0_attn_Wq': _L0_attn_in['Wq'], 'L0_attn_bq': _L0_attn_in['bq'], 'L0_attn_Wk': _L0_attn_in['Wk'], 'L0_attn_bk': _L0_attn_in['bk'], 'L0_attn_Wv': _L0_attn_in['Wv'], 'L0_attn_bv': _L0_attn_in['bv'], 'L0_attn_Wo': _L0_attn_in['Wo'], 'L0_attn_bo': _L0_attn_in['bo'], 'L0_ffn_Wg': _L0_ffn_in['Wg'], 'L0_ffn_bg': _L0_ffn_in['bg'], 'L0_ffn_Wqkv': _L0_ffn_in['Wqkv'], 'L0_ffn_bqkv': _L0_ffn_in['bqkv'], 'L0_ffn_Wproj': _L0_ffn_in['Wproj'], 'L0_ffn_bproj': _L0_ffn_in['bproj'], 'L0_ffn_A': _L0_ffn_in['A'], 'L0_ffn_ba': _L0_ffn_in['ba'], 'L0_ffn_Bm': _L0_ffn_in['Bm'], 'L0_ffn_bb': _L0_ffn_in['bb']}

def reference(x, L0_tok_W, L0_tok_b, L0_tok_pos_emb, L0_attn_Wq, L0_attn_bq, L0_attn_Wk, L0_attn_bk, L0_attn_Wv, L0_attn_bv, L0_attn_Wo, L0_attn_bo, L0_ffn_Wg, L0_ffn_bg, L0_ffn_Wqkv, L0_ffn_bqkv, L0_ffn_Wproj, L0_ffn_bproj, L0_ffn_A, L0_ffn_ba, L0_ffn_Bm, L0_ffn_bb):
    import jax
    import jax.numpy as jnp

    def _L0_tok_ref(x, W, b, pos_emb):
        import jax, jax.numpy as jnp
        import numpy as np
        IMG = 64
        PATCH = 16
        C = 3
        D = 192
        NP_ = (IMG // PATCH) ** 2
        B = 64

        def _patchify(x):
            Bn, H, Wd, Cn = x.shape
            hp, wp = (H // PATCH, Wd // PATCH)
            x = x.reshape(Bn, hp, PATCH, wp, PATCH, Cn)
            x = x.transpose(0, 1, 3, 2, 4, 5)
            return x.reshape(Bn, hp * wp, PATCH * PATCH * Cn)
        patches = _patchify(x)
        proj = jnp.einsum('bnd,de->bne', patches, W) + b
        return proj + pos_emb[None, :, :]

    def _L0_attn_ref(x, Wq, bq, Wk, bk, Wv, bv, Wo, bo):
        import jax, jax.numpy as jnp
        import numpy as np
        EMBED_DIM = 192
        NUM_HEADS = 12
        HEAD_DIM = EMBED_DIM // NUM_HEADS
        SEG_LEN = 64
        DILATION = 1

        def _dilated_mask(seq_len):
            idx = jnp.arange(seq_len)
            seg_id = idx // SEG_LEN
            on_stride = idx % SEG_LEN % DILATION == 0
            valid = (seg_id[:, None] == seg_id[None, :]) & on_stride[:, None] & on_stride[None, :]
            return jnp.where(valid, 0.0, -jnp.inf).astype(jnp.float32)
        B, S, E = x.shape
        H, D = (NUM_HEADS, HEAD_DIM)

        def proj(W, b):
            return (x @ W.T + b).reshape(B, S, H, D).transpose(0, 2, 1, 3)
        q = proj(Wq, bq)
        k = proj(Wk, bk)
        v = proj(Wv, bv)
        mask = _dilated_mask(S)
        scores = jnp.einsum('bhqd,bhkd->bhqk', q, k) / jnp.sqrt(jnp.float32(D))
        attn = jax.nn.softmax(scores + mask, axis=-1)
        ctx = jnp.einsum('bhqk,bhkd->bhqd', attn, v)
        ctx = ctx.transpose(0, 2, 1, 3).reshape(B, S, E)
        return ctx @ Wo.T + bo

    def _L0_ffn_ref(x, Wg, bg, Wqkv, bqkv, Wproj, bproj, A, ba, Bm, bb):
        import jax, jax.numpy as jnp
        import numpy as np
        DIM = 192
        NUM_HEADS = 12
        HEAD_DIM = DIM // NUM_HEADS
        SCALE = HEAD_DIM ** (-0.5)
        NUM_EXPERTS = 8
        RANK = 16
        ALPHA = 32
        TOPK = 2
        SCALING = ALPHA / RANK
        B, S = (8, 256)
        b, s, d = x.shape
        t = b * s
        xf = x.reshape(t, d)
        probs = jax.nn.softmax(xf @ Wg.T + bg, axis=-1)
        top_w, top_idx = jax.lax.top_k(probs, TOPK)
        combine = jnp.zeros((t, NUM_EXPERTS), x.dtype).at[jnp.arange(t)[:, None], top_idx].add(top_w)
        h = jnp.einsum('td,erd->ter', xf, A) + ba
        hw = h * combine[:, :, None]
        delta = jnp.einsum('ter,eor->to', hw, Bm) + combine @ bb
        delta = delta * SCALING
        qkv = xf @ Wqkv.T + bqkv + delta
        qkv = qkv.reshape(b, s, 3, NUM_HEADS, HEAD_DIM)
        qkv = jnp.transpose(qkv, (2, 0, 3, 1, 4))
        q, k, v = (qkv[0], qkv[1], qkv[2])
        attn = jax.nn.softmax(jnp.einsum('bhsd,bhtd->bhst', q, k) * SCALE, axis=-1)
        out = jnp.einsum('bhst,bhtd->bhsd', attn, v)
        out = jnp.transpose(out, (0, 2, 1, 3)).reshape(b, s, d)
        return out @ Wproj.T + bproj
    h = _L0_tok_ref(x, L0_tok_W, L0_tok_b, L0_tok_pos_emb)
    h = _layernorm(h + _L0_attn_ref(h, L0_attn_Wq, L0_attn_bq, L0_attn_Wk, L0_attn_bk, L0_attn_Wv, L0_attn_bv, L0_attn_Wo, L0_attn_bo), axis=-1)
    h = _layernorm(h + _L0_ffn_ref(h, L0_ffn_Wg, L0_ffn_bg, L0_ffn_Wqkv, L0_ffn_bqkv, L0_ffn_Wproj, L0_ffn_bproj, L0_ffn_A, L0_ffn_ba, L0_ffn_Bm, L0_ffn_bb), axis=-1)
    return h

_drawn_inputs = setup_inputs


def setup_inputs(seed=0):
    import zlib

    import numpy as np

    out = dict(_drawn_inputs(seed))
    spreads = {'L0_tok_b': (0.0, 0.1)}
    factors = {'L0_tok_pos_emb': 2.804,
     'L0_attn_Wq': 8.0,
     'L0_attn_bq': 8.0,
     'L0_attn_Wk': 8.0,
     'L0_attn_bk': 64.0,
     'L0_attn_bv': 8.0,
     'L0_ffn_Wg': 8.0,
     'L0_ffn_bg': 8.0,
     'L0_ffn_Wqkv': 2.791,
     'L0_ffn_bqkv': 8.0,
     'L0_ffn_bproj': 10.948,
     'L0_ffn_A': 8.0,
     'L0_ffn_ba': 8.0,
     'L0_ffn_Bm': 8.0,
     'L0_ffn_bb': 8.0}
    for name, (base, spread) in spreads.items():
        noise = np.random.default_rng([zlib.crc32(name.encode()), seed]).standard_normal(out[name].shape)
        drawn = base * np.exp(spread * noise) if base else spread * noise
        out[name] = jnp.asarray(drawn.astype(out[name].dtype))
    for name, factor in factors.items():
        out[name] = (out[name] * factor).astype(out[name].dtype)
    return out
```

```python
from contextlib import ExitStack

import concourse.bass as bass
from concourse import mybir

F32 = mybir.dt.float32
ALU = mybir.AluOpType
ACT = mybir.ActivationFunctionType
AX_X = mybir.AxisListType.X

P = 128
IMAGES, SIDE, PATCH, CH = 32, 64, 16, 3
NTOK = (SIDE // PATCH) ** 2
D = 192
HEADS = 12
HD = D // HEADS
TOKENS = IMAGES * NTOK
TILES = TOKENS // P
UNITS = 2 * TILES
PIX = PATCH * PATCH * CH
FC = PIX // P
HALF = D // 2
ONE = HALF
PAIR = 2 * NTOK
PAIRS = P // PAIR
HA = P // HD
HB = HEADS - HA
DB = D - P
EXPERTS, RANK = 8, 16
ER = EXPERTS * RANK
LORA_SCALE = 2.0
ATT_SCALE = HD ** -0.5
EPS = 1e-5
HQ = P // PAIR
HC = HEADS // HQ
NEG = -3.0e38
TAKEN = -2.0e38
QKC, VC, OC = 0, 3 * P, 3 * P + D
WC = OC + D


def slots():
    yield "embed", 0
    yield "turn_h", 0
    yield "embed", 1
    for t in range(UNITS + 2):
        for stage, u in (("turn_ctx", t - 2), ("project", t), ("turn_probs", t - 1), ("turn_h", t + 1),
                         ("output", t - 2), ("gate", t + 1), ("context", t - 1), ("scores", t),
                         ("embed", t + 2), ("turn_gated", t + 1)):
            if not 0 <= u < UNITS:
                continue
            if stage in ("gate", "turn_gated") and u < TILES:
                continue
            if stage == "embed" and u >= TILES:
                continue
            yield stage, u


def tower(nc, xT_d, wtok_d, posb_d, w1_d, w2_d, gw_d, lb_d, out_d):
    with ExitStack() as ctx:
        def sb(name, shape):
            return ctx.enter_context(nc.sbuf_tensor(name, shape, F32))

        def bank(name):
            return ctx.enter_context(nc.psum_tensor(name, [P, 512], F32))

        def sem(name):
            return ctx.enter_context(nc.semaphore(name))

        xT = sb("xT", [P, TILES, FC, P])
        wtok = sb("wtok", [P, FC, D])
        posb = sb("posb", [P, 2, D])
        pos = sb("pos", [P, D])
        w1 = sb("w1", [ONE + 1, 2, WC])
        w2 = sb("w2", [HALF + EXPERTS, 2, WC])
        gw = sb("gw", [ONE + 1, 2, ER + EXPERTS])
        lb = sb("lb", [P, 3 * P + D])
        ident = sb("ident", [P, P])
        head_mask = sb("head_mask", [P, HA])
        first = sb("first", [P, 2])
        second = sb("second", [P, 2])
        minus_half = sb("minus_half", [P, 1])
        h = sb("h", [P, UNITS + TILES, D])
        hT = sb("hT", [HALF + EXPERTS, UNITS, 2, P])
        qk = sb("qk", [P, UNITS, 2, P])
        q2 = sb("q2", [DB, UNITS, P])
        k2 = sb("k2", [DB, UNITS, P])
        kxa = sb("kxa", [P, 2, HA, P])
        kxb = sb("kxb", [DB, 2, HB, P])
        vx = sb("vx", [P, 2, PAIRS, HC, HQ, HD])
        lo = sb("lo", [P, UNITS, HEADS, NTOK])
        sc = sb("sc", [P, UNITS, HEADS, NTOK])
        top = sb("top", [P, UNITS, HEADS])
        den = sb("den", [P, UNITS, HEADS])
        rden = sb("rden", [P, UNITS, HEADS])
        ex = sb("ex", [P, UNITS, HEADS, NTOK])
        prob = sb("prob", [P, UNITS, HEADS, 2, NTOK])
        probT = sb("probT", [P, UNITS, HC, P])
        cx = sb("cx", [P, UNITS, D])
        cxT = sb("cxT", [ONE + 1, UNITS, 2, P])
        y = sb("y", [P, UNITS, D])
        st = sb("st", [P, UNITS, 6])
        mv = sb("mv", [P, UNITS, 2])
        veps = sb("veps", [P, UNITS, 1])
        rstd = sb("rstd", [P, UNITS, 1])
        lg = sb("lg", [P, TILES, 2 * EXPERTS])
        t8 = sb("t8", [P, TILES, 8])
        rep = sb("rep", [P, TILES, 8])
        zap = sb("zap", [P, TILES, 2 * EXPERTS])
        chosen = sb("chosen", [P, TILES, EXPERTS])
        nmax = sb("nmax", [P, TILES, 1])
        ge = sb("ge", [P, TILES, EXPERTS])
        gsum = sb("gsum", [P, TILES, 1])
        grec = sb("grec", [P, TILES, 1])
        comb = sb("comb", [P, TILES, EXPERTS])
        hw = sb("hw", [P, TILES, EXPERTS, RANK])
        hwT = sb("hwT", [P, TILES, P])

        QK, V, S, PT, CX, T, Y, G = [bank("ps_" + n) for n in ("qk", "v", "s", "pt", "cx", "t", "y", "g")]

        x_in = [sem(f"x_in{g}") for g in range(TILES)]
        wtok_in, posb_in, w1_in, w2_in, gw_in, lb_in = [
            sem(n) for n in ("wtok_in", "posb_in", "w1_in", "w2_in", "gw_in", "lb_in")]
        zero_id, ident_ok, hmask_ok, ones_ok, zero_v, pads_ok, pos_ok, half_ok = [
            sem(n) for n in ("zero_id", "ident_ok", "hmask_ok", "ones_ok", "zero_v", "pads_ok", "pos_ok", "half_ok")]
        emb_ps, hT_ps, qk_ps, v_ps, s_ps, pT_ps, cx_ps, cT_ps, y_ps, g_ps, gT_ps = [
            sem(n) for n in ("emb_ps", "hT_ps", "qk_ps", "v_ps", "s_ps", "pT_ps", "cx_ps", "cT_ps", "y_ps",
                             "g_ps", "gT_ps")]
        hT_ok, qk_ok, va_ok, lo_ok, ex_ok, pa_ok, pT_ok, cT_ok, ge_ok, gT_ok = [
            sem(n) for n in ("hT_ok", "qk_ok", "va_ok", "lo_ok", "ex_ok", "pa_ok", "pT_ok", "cT_ok",
                             "ge_ok", "gT_ok")]
        h_ok, kxa_ok, vb_ok, sc_ok, top_ok, sub_ok, pb_ok, den_ok, rden_ok, cx_ok, y_ok, st_ok, mv_ok, rstd_ok = [
            sem(n) for n in ("h_ok", "kxa_ok", "vb_ok", "sc_ok", "top_ok", "sub_ok", "pb_ok", "den_ok",
                             "rden_ok", "cx_ok", "y_ok", "st_ok", "mv_ok", "rstd_ok")]
        lg_ok, t8_ok, nmax_ok, rep_ok, zap_ok, chosen_ok, grec_ok, comb_ok, hw_ok = [
            sem(n) for n in ("lg_ok", "t8_ok", "nmax_ok", "rep_ok", "zap_ok", "chosen_ok", "grec_ok",
                             "comb_ok", "hw_ok")]
        kxb_ok, veps_ok, power_ok = [sem(n) for n in ("kxb_ok", "veps_ok", "power_ok")]
        out_done = sem("out_done")

        def v_part(m, a):
            return V[32 * m:32 * m + 32, 0:D].rearrange("p (c a d) -> p c a d", c=HC, a=HQ)[:, :, a, :]

        def score_part(i):
            return S[:, 0:HEADS * PAIR].rearrange("p (h i k) -> p h i k", h=HEADS, i=2)[:, :, i, :]

        block = ctx.enter_context(nc.Block())

        @block.sync
        def _(sp):
            sp.dma_start(xT[:, 0], xT_d[0]).then_inc(x_in[0], 16)
            sp.dma_start(w1[:], w1_d).then_inc(w1_in, 16)
            for g in range(1, TILES):
                sp.dma_start(xT[:, g], xT_d[g]).then_inc(x_in[g], 16)
            sp.dma_start(w2[:], w2_d).then_inc(w2_in, 16)
            for g in range(TILES):
                sp.wait_ge(h_ok, UNITS + g + 1)
                sp.dma_start(out_d[g * P:(g + 1) * P, :], h[:, UNITS + g]).then_inc(out_done, 16)
            sp.wait_ge(out_done, 16 * TILES)

        @block.gpsimd
        def _(pool):
            pool.memset(ident[:], 0.0).then_inc(zero_id, 1)
            pool.memset(head_mask[:], 1.0).then_inc(zero_id, 1)
            pool.wait_ge(zero_id, 1)
            pool.affine_select(out=ident[:], in_=ident[:], compare_op=ALU.not_equal, fill=1.0, base=0,
                               pattern=[[-1, P]], channel_multiplier=1).then_inc(ident_ok, 1)
            pool.wait_ge(zero_id, 2)
            pool.affine_select(out=head_mask[:], in_=head_mask[:], compare_op=ALU.is_ge, fill=0.0, base=0,
                               pattern=[[-HD, HA]], channel_multiplier=1).then_inc(hmask_ok, 1)
            pool.wait_ge(hmask_ok, 1)
            pool.affine_select(out=head_mask[:], in_=head_mask[:], compare_op=ALU.is_ge, fill=0.0, base=HD - 1,
                               pattern=[[HD, HA]], channel_multiplier=-1).then_inc(hmask_ok, 1)
            pool.memset(vx[:], 0.0).then_inc(zero_v, 1)
            pool.memset(minus_half[:], -0.5).then_inc(power_ok, 1)
            pool.wait_ge(hmask_ok, 2)
            pool.wait_ge(power_ok, 1)

            def spread_keys(u):
                pool.wait_ge(qk_ok, u + 1)
                if u >= 2:
                    pool.wait_ge(s_ps, u - 1)
                pool.tensor_tensor(kxb[:, u % 2], k2[:, u].unsqueeze(1).to_broadcast([DB, HB, P]),
                                   head_mask[0:DB, 0:HB].unsqueeze(2).to_broadcast([DB, HB, P]),
                                   ALU.mult).then_inc(kxb_ok, 1)

            def deviation(u):
                pool.wait_ge(mv_ok, u + 1)
                pool.tensor_scalar(veps[:, u], mv[:, u, 1:2], EPS, None, ALU.add).then_inc(veps_ok, 1)
                pool.wait_ge(veps_ok, u + 1)
                pool.tensor_tensor(rstd[:, u], veps[:, u], minus_half[:], ALU.pow).then_inc(rstd_ok, 1)

            for t in range(UNITS + 2):
                if t < UNITS:
                    spread_keys(t)
                if 0 <= t - 2:
                    deviation(t - 2)

        @block.scalar
        def _(act):
            act.dma_start(wtok[:], wtok_d).then_inc(wtok_in, 16)
            act.dma_start(posb[:], posb_d).then_inc(posb_in, 16)
            act.dma_start(gw[:], gw_d).then_inc(gw_in, 16)
            act.dma_start(lb[:], lb_d).then_inc(lb_in, 16)

            def turned_h(u):
                act.wait_ge(hT_ps, u + 1)
                act.activation(hT[0:HALF, u], T[0:HALF, 0:2 * P].rearrange("p (c t) -> p c t", c=2),
                               ACT.Copy).then_inc(hT_ok, 1)

            def queries_keys(u):
                act.wait_ge(qk_ps, u + 1)
                act.activation(qk[:, u], QK[:, 0:2 * P].rearrange("p (c t) -> p c t", c=2), ACT.Copy)
                act.activation(q2[:, u], QK[0:DB, 2 * P:3 * P], ACT.Copy)
                act.activation(k2[:, u], QK[DB:P, 2 * P:3 * P], ACT.Copy).then_inc(qk_ok, 1)

            def values(u):
                act.wait_ge(v_ps, u + 1)
                act.wait_ge(zero_v, 1)
                if u >= 2:
                    act.wait_ge(cx_ps, u - 1)
                for m in range(PAIRS // 2):
                    for a in range(HQ):
                        last = act.activation(vx[32 * a:32 * a + 32, u % 2, m, :, a, :], v_part(m, a), ACT.Copy)
                last.then_inc(va_ok, 1)

            def low_scores(u):
                act.wait_ge(s_ps, u + 1)
                act.wait_ge(half_ok, 4)
                act.activation(lo[:, u], score_part(0), ACT.Copy, scale=first[:, 1:2]).then_inc(lo_ok, 1)

            def exps(u):
                act.wait_ge(sub_ok, u + 1)
                act.activation(ex[:, u], sc[:, u], ACT.Exp).then_inc(ex_ok, 1)
                act.wait_ge(ex_ok, u + 1)
                act.activation(prob[:, u, :, 0, :], ex[:, u], ACT.Copy, scale=first[:, 0:1]).then_inc(pa_ok, 1)

            def turned_probs(u):
                act.wait_ge(pT_ps, u + 1)
                act.activation(probT[:, u], PT[:, 0:HC * P].rearrange("p (c t) -> p c t", c=HC),
                               ACT.Copy).then_inc(pT_ok, 1)

            def turned_ctx(u):
                act.wait_ge(cT_ps, u + 1)
                act.activation(cxT[0:HALF, u], T[0:HALF, 0:2 * P].rearrange("p (c t) -> p c t", c=2),
                               ACT.Copy).then_inc(cT_ok, 1)

            def gate_exps(u):
                g = u - TILES
                act.wait_ge(nmax_ok, g + 1)
                act.activation(ge[:, g], lg[:, g, 0:EXPERTS], ACT.Exp, bias=nmax[:, g],
                               accum_out=gsum[:, g]).then_inc(ge_ok, 1)

            def turned_gated(u):
                g = u - TILES
                act.wait_ge(gT_ps, g + 1)
                act.activation(hwT[:, g], G[:, 0:P], ACT.Copy, scale=LORA_SCALE)
                act.activation(hT[HALF:HALF + EXPERTS, u, 0, :], G[0:EXPERTS, P:2 * P], ACT.Copy,
                               scale=LORA_SCALE).then_inc(gT_ok, 1)

            turned_h(0)
            for t in range(UNITS + 2):
                if 0 <= t - 2:
                    turned_ctx(t - 2)
                if t < UNITS:
                    queries_keys(t)
                if 0 <= t - 1 < UNITS:
                    turned_probs(t - 1)
                if t + 1 < UNITS:
                    turned_h(t + 1)
                if t < UNITS:
                    values(t)
                if TILES <= t + 1 < UNITS:
                    gate_exps(t + 1)
                if t < UNITS:
                    low_scores(t)
                if TILES <= t + 1 < UNITS:
                    turned_gated(t + 1)
                if t < UNITS:
                    exps(t)

        @block.vector
        def _(dve):
            def embedded(g):
                dve.wait_ge(pos_ok, 1)
                dve.wait_ge(emb_ps, g + 1)
                dve.tensor_tensor(h[:, g], Y[:, 0:D], pos[:], ALU.add).then_inc(h_ok, 1)

            def spread_keys(u):
                dve.wait_ge(qk_ok, u + 1)
                if u >= 2:
                    dve.wait_ge(s_ps, u - 1)
                dve.tensor_tensor(kxa[:, u % 2], qk[:, u, 1].unsqueeze(1).to_broadcast([P, HA, P]),
                                  head_mask[:].unsqueeze(2).to_broadcast([P, HA, P]),
                                  ALU.mult).then_inc(kxa_ok, 1)

            def values(u):
                dve.wait_ge(v_ps, u + 1)
                dve.wait_ge(zero_v, 1)
                if u >= 2:
                    dve.wait_ge(cx_ps, u - 1)
                for m in range(PAIRS // 2, PAIRS):
                    for a in range(HQ):
                        last = dve.tensor_copy(vx[32 * a:32 * a + 32, u % 2, m, :, a, :], v_part(m, a))
                last.then_inc(vb_ok, 1)

            def scores(u):
                dve.wait_ge(lo_ok, u + 1)
                dve.scalar_tensor_tensor(out=sc[:, u], in0=score_part(1), scalar=second[:, 1:2], in1=lo[:, u],
                                         op0=ALU.mult, op1=ALU.add).then_inc(sc_ok, 1)
                dve.wait_ge(sc_ok, u + 1)
                dve.tensor_reduce(top[:, u], sc[:, u], AX_X, ALU.max).then_inc(top_ok, 1)
                dve.wait_ge(top_ok, u + 1)
                dve.tensor_tensor(sc[:, u], sc[:, u], top[:, u].unsqueeze(2).to_broadcast([P, HEADS, NTOK]),
                                  ALU.subtract).then_inc(sub_ok, 1)

            def probs(u):
                dve.wait_ge(ex_ok, u + 1)
                dve.tensor_scalar(prob[:, u, :, 1, :], ex[:, u], second[:, 0:1], None, ALU.mult).then_inc(pb_ok, 1)
                dve.tensor_reduce(den[:, u], ex[:, u], AX_X, ALU.add).then_inc(den_ok, 1)
                dve.wait_ge(den_ok, u + 1)
                dve.reciprocal(rden[:, u], den[:, u]).then_inc(rden_ok, 1)

            def context(u):
                dve.wait_ge(cx_ps, u + 1)
                dve.wait_ge(rden_ok, u + 1)
                dve.tensor_tensor(cx[:, u].rearrange("p (h d) -> p h d", h=HEADS),
                                  CX[:, 0:D].rearrange("p (h d) -> p h d", h=HEADS),
                                  rden[:, u].unsqueeze(2).to_broadcast([P, HEADS, HD]),
                                  ALU.mult).then_inc(cx_ok, 1)

            def norm(u):
                dve.wait_ge(y_ps, u + 1)
                dve.wait_ge(h_ok, u + 1)
                dve.tensor_tensor(y[:, u], Y[:, 0:D], h[:, u], ALU.add).then_inc(y_ok, 1)
                dve.wait_ge(y_ok, u + 1)
                dve.bn_stats(st[:, u], y[:, u]).then_inc(st_ok, 1)
                dve.wait_ge(st_ok, u + 1)
                dve.bn_aggr(mv[:, u], st[:, u]).then_inc(mv_ok, 1)

            def normed(u):
                dve.wait_ge(rstd_ok, u + 1)
                dve.tensor_scalar(h[:, u + TILES], y[:, u], mv[:, u, 0:1], rstd[:, u], ALU.subtract,
                                  ALU.mult).then_inc(h_ok, 1)

            def gate(u):
                g = u - TILES
                dve.wait_ge(pads_ok, 3)
                dve.wait_ge(g_ps, g + 1)
                dve.tensor_copy(lg[:, g, 0:EXPERTS], G[:, ER:ER + EXPERTS]).then_inc(lg_ok, 1)
                dve.wait_ge(lg_ok, g + 1)
                dve.max(t8[:, g], lg[:, g, 0:EXPERTS]).then_inc(t8_ok, 1)
                dve.wait_ge(t8_ok, g + 1)
                dve.tensor_scalar(nmax[:, g], t8[:, g, 0:1], -1.0, None, ALU.mult).then_inc(nmax_ok, 1)
                dve.tensor_copy(rep[:, g, 0:2], t8[:, g, 0:2]).then_inc(rep_ok, 1)
                dve.wait_ge(rep_ok, g + 1)
                dve.match_replace(out=zap[:, g], in_to_replace=rep[:, g], in_values=lg[:, g],
                                  imm_value=TAKEN).then_inc(zap_ok, 1)
                dve.wait_ge(zap_ok, g + 1)
                dve.tensor_tensor(chosen[:, g], zap[:, g, 0:EXPERTS], lg[:, g, 0:EXPERTS],
                                  ALU.not_equal).then_inc(chosen_ok, 1)
                dve.wait_ge(ge_ok, g + 1)
                dve.reciprocal(grec[:, g], gsum[:, g]).then_inc(grec_ok, 1)
                dve.wait_ge(grec_ok, g + 1)
                dve.wait_ge(chosen_ok, g + 1)
                dve.scalar_tensor_tensor(out=comb[:, g], in0=ge[:, g], scalar=grec[:, g], in1=chosen[:, g],
                                         op0=ALU.mult, op1=ALU.mult).then_inc(comb_ok, 1)
                dve.wait_ge(comb_ok, g + 1)
                dve.tensor_tensor(hw[:, g], G[:, 0:ER].rearrange("p (e r) -> p e r", e=EXPERTS),
                                  comb[:, g].unsqueeze(2).to_broadcast([P, EXPERTS, RANK]),
                                  ALU.mult).then_inc(hw_ok, 1)

            dve.memset(hT[ONE:ONE + 1, :, 1, :], 1.0).then_inc(ones_ok, 1)
            dve.memset(cxT[ONE:ONE + 1, :, 1, :], 1.0).then_inc(ones_ok, 1)
            dve.memset(lg[:], NEG).then_inc(pads_ok, 1)
            dve.memset(rep[:], NEG).then_inc(pads_ok, 1)
            dve.memset(zap[:], NEG).then_inc(pads_ok, 1)
            dve.wait_ge(posb_in, 16)
            dve.tensor_tensor(pos[:], posb[:, 0], posb[:, 1], ALU.add).then_inc(pos_ok, 1)
            embedded(0)
            dve.wait_ge(hmask_ok, 2)
            dve.tensor_reduce(first[:, 0:1], head_mask[:, 0:HA:2], AX_X, ALU.add).then_inc(half_ok, 1)
            dve.tensor_reduce(second[:, 0:1], head_mask[:, 1:HA:2], AX_X, ALU.add).then_inc(half_ok, 1)
            dve.wait_ge(half_ok, 2)
            dve.tensor_scalar(first[:, 1:2], first[:, 0:1], ATT_SCALE, None, ALU.mult).then_inc(half_ok, 1)
            dve.tensor_scalar(second[:, 1:2], second[:, 0:1], ATT_SCALE, None, ALU.mult).then_inc(half_ok, 1)
            embedded(1)
            for t in range(UNITS + 2):
                if t < UNITS:
                    spread_keys(t)
                if 0 <= t - 2:
                    norm(t - 2)
                if TILES <= t + 1 < UNITS:
                    gate(t + 1)
                if 0 <= t - 1 < UNITS:
                    context(t - 1)
                if t < UNITS:
                    values(t)
                if 0 <= t - 2:
                    normed(t - 2)
                if t < UNITS:
                    scores(t)
                if t + 2 < TILES:
                    embedded(t + 2)
                if t < UNITS:
                    probs(t)

        @block.tensor
        def _(pe):
            def embed(g):
                pe.wait_ge(x_in[g], 16)
                if g == 0:
                    pe.wait_ge(wtok_in, 16)
                if g >= 1:
                    pe.wait_ge(h_ok, g)
                for c in range(FC):
                    last = pe.matmul(Y[:, 0:D], xT[:, g, c, :], wtok[:, c, :], start=(c == 0), stop=(c == FC - 1))
                last.then_inc(emb_ps, 1)

            def turn_h(u):
                pe.wait_ge(ident_ok, 1)
                pe.wait_ge(h_ok, u + 1)
                if u >= 3:
                    pe.wait_ge(cT_ok, u - 2)
                elif u >= 1:
                    pe.wait_ge(hT_ok, u)
                for c in range(2):
                    last = pe.transpose(T[0:HALF, c * P:(c + 1) * P], h[:, u, c * HALF:(c + 1) * HALF], ident[:])
                last.then_inc(hT_ps, 1)

            def gate(u):
                g = u - TILES
                pe.wait_ge(hT_ok, u + 1)
                if g == 0:
                    pe.wait_ge(gw_in, 16)
                else:
                    pe.wait_ge(gT_ok, g)
                for c, rows in enumerate((HALF, ONE + 1)):
                    last = pe.matmul(G[:, 0:ER + EXPERTS], hT[0:rows, u, c, :], gw[0:rows, c, :],
                                     start=(c == 0), stop=(c == 1))
                last.then_inc(g_ps, 1)

            def turn_gated(u):
                g = u - TILES
                pe.wait_ge(hw_ok, g + 1)
                pe.wait_ge(comb_ok, g + 1)
                pe.transpose(G[:, 0:P], hw[:, g].rearrange("p e r -> p (e r)"), ident[:])
                pe.transpose(G[0:EXPERTS, P:2 * P], comb[:, g], ident[:]).then_inc(gT_ps, 1)

            def project(u):
                pe.wait_ge(hT_ok, u + 1)
                if u == 0:
                    pe.wait_ge(ones_ok, 2)
                    pe.wait_ge(w1_in, 16)
                if u == TILES:
                    pe.wait_ge(w2_in, 16)
                    pe.wait_ge(lb_in, 16)
                if u >= 1:
                    pe.wait_ge(qk_ok, u)
                if u < TILES:
                    parts = [(w1[0:HALF, 0], hT[0:HALF, u, 0, :]), (w1[0:ONE + 1, 1], hT[0:ONE + 1, u, 1, :])]
                else:
                    pe.wait_ge(gT_ok, u - TILES + 1)
                    parts = [(w2[0:ONE + 1, 1], hT[0:ONE + 1, u, 1, :]),
                             (w2[0:HALF + EXPERTS, 0], hT[0:HALF + EXPERTS, u, 0, :]),
                             (lb[:], hwT[:, u - TILES, :])]
                for j in range(3):
                    for i, (w, a) in enumerate(parts):
                        last = pe.matmul(QK[:, j * P:(j + 1) * P], w[:, j * P:(j + 1) * P], a,
                                         start=(i == 0), stop=(i == len(parts) - 1))
                last.then_inc(qk_ps, 1)
                if u >= 1:
                    pe.wait_ge(va_ok, u)
                    pe.wait_ge(vb_ok, u)
                for i, (w, a) in enumerate(parts):
                    last = pe.matmul(V[:, 0:D], a, w[:, VC:VC + D], start=(i == 0), stop=(i == len(parts) - 1))
                last.then_inc(v_ps, 1)

            def scores(u):
                pe.wait_ge(qk_ok, u + 1)
                pe.wait_ge(kxa_ok, u + 1)
                if u >= 1:
                    pe.wait_ge(sc_ok, u)
                for m in range(PAIRS):
                    r = slice(32 * m, 32 * m + 32)
                    pe.matmul(S[r, 0:HA * PAIR], qk[:, u, 0, r], kxa[:, u % 2, :, r], start=True, stop=True)
                pe.wait_ge(kxb_ok, u + 1)
                for m in range(PAIRS):
                    r = slice(32 * m, 32 * m + 32)
                    last = pe.matmul(S[r, HA * PAIR:HEADS * PAIR], q2[:, u, r], kxb[:, u % 2, :, r],
                                     start=True, stop=True)
                last.then_inc(s_ps, 1)

            def turn_probs(u):
                pe.wait_ge(pa_ok, u + 1)
                pe.wait_ge(pb_ok, u + 1)
                if u >= 1:
                    pe.wait_ge(pT_ok, u)
                rows = prob[:, u].rearrange("p h i k -> p (h i k)")
                for c in range(HC):
                    last = pe.transpose(PT[:, c * P:(c + 1) * P], rows[:, c * P:(c + 1) * P], ident[:])
                last.then_inc(pT_ps, 1)

            def context(u):
                pe.wait_ge(pT_ok, u + 1)
                pe.wait_ge(va_ok, u + 1)
                pe.wait_ge(vb_ok, u + 1)
                if u >= 1:
                    pe.wait_ge(cx_ok, u)
                for c in range(HC):
                    for m in range(PAIRS):
                        r = slice(32 * m, 32 * m + 32)
                        last = pe.matmul(CX[r, c * HQ * HD:(c + 1) * HQ * HD], probT[:, u, c, r],
                                         vx[:, u % 2, m, c].rearrange("p a d -> p (a d)"), start=True, stop=True)
                last.then_inc(cx_ps, 1)

            def turn_ctx(u):
                pe.wait_ge(cx_ok, u + 1)
                pe.wait_ge(hT_ok, min(u + 3, UNITS))
                if u + 3 > UNITS:
                    pe.wait_ge(cT_ok, u)
                for c in range(2):
                    last = pe.transpose(T[0:HALF, c * P:(c + 1) * P], cx[:, u, c * HALF:(c + 1) * HALF], ident[:])
                last.then_inc(cT_ps, 1)

            def output(u):
                w = w1 if u < TILES else w2
                pe.wait_ge(cT_ok, u + 1)
                if u == 0:
                    pe.wait_ge(h_ok, TILES)
                else:
                    pe.wait_ge(y_ok, u)
                for c, rows in enumerate((HALF, ONE + 1)):
                    last = pe.matmul(Y[:, 0:D], cxT[0:rows, u, c, :], w[0:rows, c, OC:OC + D],
                                     start=(c == 0), stop=(c == 1))
                last.then_inc(y_ps, 1)

            stages = {"embed": embed, "turn_h": turn_h, "gate": gate, "turn_gated": turn_gated,
                      "project": project, "scores": scores, "turn_probs": turn_probs, "context": context,
                      "turn_ctx": turn_ctx, "output": output}
            for stage, u in slots():
                stages[stage](u)


def kernel(**inputs):
    import numpy as np
    import concourse.bacc as bacc
    from concourse.bass_utils import run_bass_kernel_spmd

    a = {k: np.asarray(v) for k, v in inputs.items()}
    side = SIDE // PATCH

    x = a["x"].reshape(IMAGES, side, PATCH, side, PATCH, CH).transpose(2, 4, 5, 0, 1, 3)
    xT = x.reshape(FC, P, TILES, P).transpose(2, 1, 0, 3)
    wtok = a["L0_tok_W"].reshape(FC, P, D).transpose(1, 0, 2)
    posb = np.stack([np.tile(a["L0_tok_pos_emb"], (P // NTOK, 1)), np.broadcast_to(a["L0_tok_b"], (P, D))], 1)

    def columns(q, k, v, o):
        return np.concatenate([q[:P], k[:P], q[P:], k[P:], v, o], 0)

    def chunks(w, bias, rows):
        out = np.zeros((rows, 2, w.shape[0]), w.dtype)
        out[:HALF] = w.T.reshape(2, HALF, w.shape[0]).transpose(1, 0, 2)
        out[ONE, 1] = bias
        return out

    w1 = chunks(columns(*(a[f"L0_attn_W{n}"] for n in "qkvo")),
                columns(*(a[f"L0_attn_b{n}"] for n in "qkvo")), ONE + 1)
    wqkv, bqkv = a["L0_ffn_Wqkv"].reshape(3, D, D), a["L0_ffn_bqkv"].reshape(3, D)
    w2 = chunks(columns(*wqkv, a["L0_ffn_Wproj"]), columns(*bqkv, a["L0_ffn_bproj"]), HALF + EXPERTS)
    bb = a["L0_ffn_bb"].T.reshape(3, D, EXPERTS)
    w2[HALF:, 0, :OC] = np.concatenate([bb[0][:P], bb[1][:P], bb[0][P:], bb[1][P:], bb[2]], 0).T
    bm = a["L0_ffn_Bm"].transpose(1, 0, 2).reshape(3, D, ER)
    lb = np.concatenate([bm[0][:P], bm[1][:P], bm[0][P:], bm[1][P:], bm[2]], 0).T
    gw = chunks(np.concatenate([a["L0_ffn_A"].reshape(ER, D), a["L0_ffn_Wg"]], 0),
                np.concatenate([a["L0_ffn_ba"].reshape(ER), a["L0_ffn_bg"]], 0), ONE + 1)

    nc = bacc.Bacc("TRN2", target_bir_lowering=False, num_devices=1)
    arrays, args = {}, []
    for name, v in (("xT", xT), ("wtok", wtok), ("posb", posb), ("w1", w1), ("w2", w2), ("gw", gw), ("lb", lb)):
        v = np.ascontiguousarray(v)
        arrays[f"in_{name}"] = v
        args.append(nc.dram_tensor(f"in_{name}", v.shape, mybir.dt.from_np(v.dtype), kind="ExternalInput").ap())
    args.append(nc.dram_tensor("out_0", (TOKENS, D), F32, kind="ExternalOutput").ap())
    tower(nc, *args)
    r = run_bass_kernel_spmd(nc, [arrays], core_ids=[0])
    return r.results[0]["out_0"].reshape(IMAGES, NTOK, D)
```

```python
from contextlib import ExitStack

import concourse.bass as bass
from concourse import mybir

F32 = mybir.dt.float32
ALU = mybir.AluOpType
ACT = mybir.ActivationFunctionType
AX_X = mybir.AxisListType.X

P = 128
IMAGES, SIDE, PATCH, CH = 32, 64, 16, 3
NTOK = (SIDE // PATCH) ** 2
D = 192
HEADS = 12
HD = D // HEADS
TOKENS = IMAGES * NTOK
TILES = TOKENS // P
UNITS = 2 * TILES
PIX = PATCH * PATCH * CH
FC = PIX // P
HALF = D // 2
ONE = HALF
PAIR = 2 * NTOK
PAIRS = P // PAIR
HA = P // HD
HB = HEADS - HA
DB = D - P
EXPERTS, RANK = 8, 16
ER = EXPERTS * RANK
LORA_SCALE = 2.0
ATT_SCALE = HD ** -0.5
EPS = 1e-5
HQ = P // PAIR
HC = HEADS // HQ
HC0 = 2 * P
K1C = 2 * P
WARM = 8
NEG = -3.0e38
TAKEN = -2.0e38
VC, OC = 3 * P, 3 * P + D
WC = OC + D


def stages_of(t):
    found = (("queries_keys", t), ("embed", t + 2), ("output", t - 2), ("gate", t + 1), ("turn_probs", t - 1),
             ("values", t), ("context", t - 1), ("scores", t), ("turn_gated", t + 1), ("turn_ctx", t - 1),
             ("turn_h", t + 2))
    first = {"gate": TILES, "turn_gated": TILES}
    last = {"embed": TILES}
    return [(stage, u) for stage, u in found if first.get(stage, 0) <= u < last.get(stage, UNITS)]


DRAIN = [("queries_keys", UNITS - 1), ("values", UNITS - 1), ("scores", UNITS - 1), ("output", UNITS - 3),
         ("turn_probs", UNITS - 2), ("context", UNITS - 2), ("turn_ctx", UNITS - 2), ("turn_probs", UNITS - 1),
         ("context", UNITS - 1), ("output", UNITS - 2), ("turn_ctx", UNITS - 1), ("output", UNITS - 1)]


def tower(nc, xT_d, wtok_d, posb_d, w1_d, w2_d, gw_d, lb_d, out_d):
    with ExitStack() as ctx:
        def sb(name, shape):
            return ctx.enter_context(nc.sbuf_tensor(name, shape, F32))

        def bank(name):
            return ctx.enter_context(nc.psum_tensor(name, [P, 512], F32))

        def sem(name):
            return ctx.enter_context(nc.semaphore(name))

        xT = sb("xT", [P, TILES, FC, P])
        wtok = sb("wtok", [P, FC, D])
        posb = sb("posb", [P, 2, D])
        pos = sb("pos", [P, D])
        w1 = sb("w1", [ONE + 1, 2, WC])
        w2 = sb("w2", [HALF + EXPERTS, 2, WC])
        gw = sb("gw", [ONE + 1, 2, ER + EXPERTS])
        lb = sb("lb", [P, 3 * P + D])
        idle = ctx.enter_context(nc.sbuf_tensor("idle", [P, 512], mybir.dt.bfloat16))
        ident = sb("ident", [P, P])
        head_mask = sb("head_mask", [P, HA])
        first = sb("first", [P, 2])
        second = sb("second", [P, 2])
        minus_half = sb("minus_half", [P, 1])
        h = sb("h", [P, UNITS + TILES, D])
        hT = sb("hT", [HALF + EXPERTS, UNITS, 2, P])
        q1 = sb("q1", [P, UNITS, P])
        q2 = sb("q2", [DB, UNITS, P])
        k2 = sb("k2", [DB, UNITS, P])
        kxa = sb("kxa", [P, 2, HA, P])
        kxb = sb("kxb", [DB, 2, HB, P])
        vx = sb("vx", [P, 2, PAIRS, HC, HQ, HD + 1])
        lo = sb("lo", [P, UNITS, HEADS, NTOK])
        sc = sb("sc", [P, UNITS, HEADS, NTOK])
        top = sb("top", [P, UNITS, HEADS])
        rden = sb("rden", [P, UNITS, HEADS])
        ex = sb("ex", [P, UNITS, HEADS, NTOK])
        prob = sb("prob", [P, UNITS, HEADS, 2, NTOK])
        probT = sb("probT", [P, UNITS, HC, P])
        cx = sb("cx", [P, UNITS, D])
        cxT = sb("cxT", [ONE + 1, UNITS, 2, P])
        y = sb("y", [P, UNITS, D])
        st = sb("st", [P, UNITS, 6])
        mv = sb("mv", [P, UNITS, 2])
        veps = sb("veps", [P, UNITS, 1])
        rstd = sb("rstd", [P, UNITS, 1])
        lg = sb("lg", [P, TILES, 2 * EXPERTS])
        t8 = sb("t8", [P, TILES, 8])
        rep = sb("rep", [P, TILES, 8])
        zap = sb("zap", [P, TILES, 2 * EXPERTS])
        chosen = sb("chosen", [P, TILES, EXPERTS])
        nmax = sb("nmax", [P, TILES, 1])
        ge = sb("ge", [P, TILES, EXPERTS])
        gsum = sb("gsum", [P, TILES, 1])
        grec = sb("grec", [P, TILES, 1])
        comb = sb("comb", [P, TILES, EXPERTS])
        hw = sb("hw", [P, TILES, EXPERTS, RANK])
        hwT = sb("hwT", [P, TILES, P])

        QK, V, S, PT, CX, T, Y, G = [bank("ps_" + n) for n in ("qk", "v", "s", "pt", "cx", "t", "y", "g")]

        x_in = [sem(f"x_in{g}") for g in range(TILES)]
        x_in0b, wtok_in0b = sem("x_in0b"), sem("wtok_in0b")
        wtok_in, posb_in, w1_in, w2_in, gw_in, lb_in = [
            sem(n) for n in ("wtok_in", "posb_in", "w1_in", "w2_in", "gw_in", "lb_in")]
        zero_id, ident_ok, hmask_ok, ones_ok, zero_v, pads_ok, pos_ok, half_ok = [
            sem(n) for n in ("zero_id", "ident_ok", "hmask_ok", "ones_ok", "zero_v", "pads_ok", "pos_ok", "half_ok")]
        emb_ps, hT_ps, k1_ps, qk_ps, v_ps, s_ps, pT_ps, cx_ps, cT_ps, y_ps, g_ps, gT_ps = [
            sem(n) for n in ("emb_ps", "hT_ps", "k1_ps", "qk_ps", "v_ps", "s_ps", "pT_ps", "cx_ps", "cT_ps", "y_ps",
                             "g_ps", "gT_ps")]
        hT_ok, k2_ok, q_ok, v_ok, lo_ok, ex_ok, pa_ok, pT_ok, cT_ok, ge_ok, gT_ok = [
            sem(n) for n in ("hT_ok", "k2_ok", "q_ok", "v_ok", "lo_ok", "ex_ok", "pa_ok", "pT_ok", "cT_ok",
                             "ge_ok", "gT_ok")]
        emb_ok, kxa_ok, sc_ok, top_ok, sub_ok, pb_ok, rden_ok, cx_ok, y_ok, st_ok, mv_ok, norm_ok = [
            sem(n) for n in ("emb_ok", "kxa_ok", "sc_ok", "top_ok", "sub_ok", "pb_ok",
                             "rden_ok", "cx_ok", "y_ok", "st_ok", "mv_ok", "norm_ok")]
        lg_ok, t8_ok, nmax_ok, rep_ok, zap_ok, chosen_ok, grec_ok, comb_ok, hw_ok = [
            sem(n) for n in ("lg_ok", "t8_ok", "nmax_ok", "rep_ok", "zap_ok", "chosen_ok", "grec_ok",
                             "comb_ok", "hw_ok")]
        kxb_ok, veps_ok, rstd_ok, power_ok = [sem(n) for n in ("kxb_ok", "veps_ok", "rstd_ok", "power_ok")]
        warm_ok = sem("warm_ok")
        out_done = sem("out_done")

        def turning_bank(u):
            return G if u == 1 else T

        def embedding_bank(g):
            return V if g == 1 else Y

        def v_part(m, a):
            return V[32 * m:32 * m + 32, 0:D].rearrange("p (c a d) -> p c a d", c=HC, a=HQ)[:, :, a, :]

        def score_part(i):
            return S[:, 0:HEADS * PAIR].rearrange("p (h i k) -> p h i k", h=HEADS, i=2)[:, :, i, :]

        block = ctx.enter_context(nc.Block())

        @block.sync
        def _(sp):
            for i in range(2):
                sp.dma_start(xT[:, 0, i * FC // 2:(i + 1) * FC // 2], xT_d[0, :, i * FC // 2:(i + 1) * FC // 2])\
                  .then_inc(x_in[0] if i == 0 else x_in0b, 16)
            sp.dma_start(xT[:, 1], xT_d[1]).then_inc(x_in[1], 16)
            sp.dma_start(w1[:], w1_d).then_inc(w1_in, 16)
            for g in range(2, TILES):
                sp.dma_start(xT[:, g], xT_d[g]).then_inc(x_in[g], 16)
            sp.dma_start(w2[:], w2_d).then_inc(w2_in, 16)
            for g in range(TILES):
                sp.wait_ge(norm_ok, TILES + g + 1)
                sp.dma_start(out_d[g * P:(g + 1) * P, :], h[:, UNITS + g]).then_inc(out_done, 16)
            sp.wait_ge(out_done, 16 * TILES)

        @block.gpsimd
        def _(pool):
            pool.memset(ident[:], 0.0).then_inc(zero_id, 1)
            pool.memset(head_mask[:], 1.0).then_inc(zero_id, 1)
            pool.wait_ge(zero_id, 1)
            pool.affine_select(out=ident[:], in_=ident[:], compare_op=ALU.not_equal, fill=1.0, base=0,
                               pattern=[[-1, P]], channel_multiplier=1).then_inc(ident_ok, 1)
            pool.wait_ge(zero_id, 2)
            pool.affine_select(out=head_mask[:], in_=head_mask[:], compare_op=ALU.is_ge, fill=0.0, base=0,
                               pattern=[[-HD, HA]], channel_multiplier=1).then_inc(hmask_ok, 1)
            pool.wait_ge(hmask_ok, 1)
            pool.affine_select(out=head_mask[:], in_=head_mask[:], compare_op=ALU.is_ge, fill=0.0, base=HD - 1,
                               pattern=[[HD, HA]], channel_multiplier=-1).then_inc(hmask_ok, 1)
            pool.memset(vx[:], 0.0).then_inc(zero_v, 1)
            pool.wait_ge(zero_v, 1)
            for a in range(HQ):
                pool.memset(vx[32 * a:32 * a + 32, :, :, :, a, HD:HD + 1].rearrange("p b m c o -> p (b m c) o"), 1.0)\
                    .then_inc(zero_v, 1)
            pool.wait_ge(zero_v, 1 + HQ)
            pool.memset(minus_half[:], -0.5).then_inc(power_ok, 1)
            pool.wait_ge(hmask_ok, 2)
            pool.wait_ge(power_ok, 1)

            def spread_keys(u):
                pool.wait_ge(k2_ok, u + 1)
                if u >= 2:
                    pool.wait_ge(s_ps, u - 1)
                pool.tensor_tensor(kxb[:, u % 2], k2[:, u].unsqueeze(1).to_broadcast([DB, HB, P]),
                                   head_mask[0:DB, 0:HB].unsqueeze(2).to_broadcast([DB, HB, P]),
                                   ALU.mult).then_inc(kxb_ok, 1)

            def deviation(u):
                pool.wait_ge(mv_ok, u + 1)
                pool.tensor_scalar(veps[:, u], mv[:, u, 1:2], EPS, None, ALU.add).then_inc(veps_ok, 1)
                pool.wait_ge(veps_ok, u + 1)
                pool.tensor_tensor(rstd[:, u], veps[:, u], minus_half[:], ALU.pow).then_inc(rstd_ok, 1)

            for t in range(UNITS + 2):
                if t < UNITS:
                    spread_keys(t)
                if t >= 2:
                    deviation(t - 2)

        @block.scalar
        def _(act):
            for i in range(2):
                act.dma_start(wtok[:, i * FC // 2:(i + 1) * FC // 2], wtok_d[:, i * FC // 2:(i + 1) * FC // 2])\
                   .then_inc(wtok_in if i == 0 else wtok_in0b, 16)
            act.dma_start(posb[:], posb_d).then_inc(posb_in, 16)
            act.dma_start(gw[:], gw_d).then_inc(gw_in, 16)
            act.dma_start(lb[:], lb_d).then_inc(lb_in, 16)

            def turned_h(u):
                act.wait_ge(hT_ps, u + 1)
                act.activation(hT[0:HALF, u], turning_bank(u)[0:HALF, HC0:HC0 + 2 * P].rearrange("p (c t) -> p c t", c=2),
                               ACT.Copy).then_inc(hT_ok, 1)

            def queries_keys(u):
                act.wait_ge(qk_ps, u + 1)
                act.activation(k2[:, u], QK[DB:P, P:2 * P], ACT.Copy).then_inc(k2_ok, 1)
                act.activation(q1[:, u], QK[:, 0:P], ACT.Copy)
                act.activation(q2[:, u], QK[0:DB, P:2 * P], ACT.Copy).then_inc(q_ok, 1)

            def values(u):
                act.wait_ge(v_ps, u + 1)
                act.wait_ge(zero_v, 1 + HQ)
                if u >= 2:
                    act.wait_ge(cx_ps, u - 1)
                for m in range(PAIRS):
                    for a in range(HQ):
                        last = act.activation(vx[32 * a:32 * a + 32, u % 2, m, :, a, 0:HD], v_part(m, a), ACT.Copy)
                last.then_inc(v_ok, 1)

            def low_scores(u):
                act.wait_ge(s_ps, u + 1)
                act.wait_ge(half_ok, 4)
                act.activation(lo[:, u], score_part(0), ACT.Copy, scale=first[:, 1:2]).then_inc(lo_ok, 1)

            def exps(u):
                act.wait_ge(sub_ok, u + 1)
                act.activation(ex[:, u], sc[:, u], ACT.Exp).then_inc(ex_ok, 1)
                act.wait_ge(ex_ok, u + 1)
                act.activation(prob[:, u, :, 0, :], ex[:, u], ACT.Copy, scale=first[:, 0:1]).then_inc(pa_ok, 1)

            def turned_probs(u):
                act.wait_ge(pT_ps, u + 1)
                act.activation(probT[:, u], PT[:, 0:HC * P].rearrange("p (c t) -> p c t", c=HC),
                               ACT.Copy).then_inc(pT_ok, 1)

            def turned_ctx(u):
                act.wait_ge(cT_ps, u + 1)
                if u + 3 < UNITS:
                    act.wait_ge(hT_ps, u + 4)
                act.activation(cxT[0:HALF, u], T[0:HALF, 0:2 * P].rearrange("p (c t) -> p c t", c=2),
                               ACT.Copy).then_inc(cT_ok, 1)

            def gate_exps(u):
                g = u - TILES
                act.wait_ge(nmax_ok, g + 1)
                act.activation(ge[:, g], lg[:, g, 0:EXPERTS], ACT.Exp, bias=nmax[:, g],
                               accum_out=gsum[:, g]).then_inc(ge_ok, 1)

            def turned_gated(u):
                g = u - TILES
                act.wait_ge(gT_ps, g + 1)
                act.activation(hwT[:, g], G[:, 0:P], ACT.Copy, scale=LORA_SCALE)
                act.activation(hT[HALF:HALF + EXPERTS, u, 0, :], G[0:EXPERTS, P:2 * P], ACT.Copy,
                               scale=LORA_SCALE).then_inc(gT_ok, 1)

            turned_h(0)
            turned_h(1)
            for t in range(UNITS - 1):
                gated = TILES <= t + 1 < UNITS
                queries_keys(t)
                if t >= 1:
                    turned_probs(t - 1)
                if gated:
                    gate_exps(t + 1)
                values(t)
                low_scores(t)
                if gated:
                    turned_gated(t + 1)
                if t >= 1:
                    turned_ctx(t - 1)
                if t + 2 < UNITS:
                    turned_h(t + 2)
                exps(t)
            u = UNITS - 1
            queries_keys(u)
            values(u)
            turned_probs(u - 1)
            exps(u)
            turned_ctx(u - 1)
            turned_probs(u)
            turned_ctx(u)

        @block.vector
        def _(dve):
            def embedded(g):
                dve.wait_ge(pos_ok, 1)
                dve.wait_ge(emb_ps, g + 1)
                dve.tensor_tensor(h[:, g], embedding_bank(g)[:, 0:D], pos[:], ALU.add).then_inc(emb_ok, 1)

            def spread_keys(u):
                dve.wait_ge(k1_ps, u + 1)
                if u >= 2:
                    dve.wait_ge(s_ps, u - 1)
                dve.tensor_tensor(kxa[:, u % 2], CX[:, K1C:K1C + P].unsqueeze(1).to_broadcast([P, HA, P]),
                                  head_mask[:].unsqueeze(2).to_broadcast([P, HA, P]),
                                  ALU.mult).then_inc(kxa_ok, 1)

            def low_scores(u):
                dve.wait_ge(s_ps, u + 1)
                dve.tensor_scalar(lo[:, u], score_part(0), first[:, 1:2], None, ALU.mult).then_inc(lo_ok, 1)

            def scores(u):
                dve.wait_ge(lo_ok, u + 1)
                dve.scalar_tensor_tensor(out=sc[:, u], in0=score_part(1), scalar=second[:, 1:2], in1=lo[:, u],
                                         op0=ALU.mult, op1=ALU.add).then_inc(sc_ok, 1)
                dve.wait_ge(sc_ok, u + 1)
                dve.tensor_reduce(top[:, u], sc[:, u], AX_X, ALU.max).then_inc(top_ok, 1)
                dve.wait_ge(top_ok, u + 1)
                dve.tensor_tensor(sc[:, u], sc[:, u], top[:, u].unsqueeze(2).to_broadcast([P, HEADS, NTOK]),
                                  ALU.subtract).then_inc(sub_ok, 1)

            def probs(u):
                dve.wait_ge(ex_ok, u + 1)
                dve.tensor_scalar(prob[:, u, :, 1, :], ex[:, u], second[:, 0:1], None, ALU.mult).then_inc(pb_ok, 1)

            def ctx_part():
                return CX[:, 0:HEADS * (HD + 1)].rearrange("p (h d) -> p h d", h=HEADS)

            def denominators(u):
                dve.wait_ge(cx_ps, u + 1)
                dve.reciprocal(rden[:, u].unsqueeze(2), ctx_part()[:, :, HD:HD + 1]).then_inc(rden_ok, 1)

            def context(u):
                dve.wait_ge(rden_ok, u + 1)
                dve.tensor_tensor(cx[:, u].rearrange("p (h d) -> p h d", h=HEADS), ctx_part()[:, :, 0:HD],
                                  rden[:, u].unsqueeze(2).to_broadcast([P, HEADS, HD]),
                                  ALU.mult).then_inc(cx_ok, 1)

            def residual(u):
                dve.wait_ge(y_ps, u + 1)
                if u < TILES:
                    dve.wait_ge(emb_ok, u + 1)
                else:
                    dve.wait_ge(norm_ok, u - TILES + 1)
                dve.tensor_tensor(y[:, u], Y[:, 0:D], h[:, u], ALU.add).then_inc(y_ok, 1)

            def moments(u):
                dve.wait_ge(y_ok, u + 1)
                dve.bn_stats(st[:, u], y[:, u]).then_inc(st_ok, 1)

            def mean_variance(u):
                dve.wait_ge(st_ok, u + 1)
                dve.bn_aggr(mv[:, u], st[:, u]).then_inc(mv_ok, 1)

            def normed(u):
                dve.wait_ge(rstd_ok, u + 1)
                dve.tensor_scalar(h[:, u + TILES], y[:, u], mv[:, u, 0:1], rstd[:, u], ALU.subtract,
                                  ALU.mult).then_inc(norm_ok, 1)

            def greatest(u):
                g = u - TILES
                dve.wait_ge(pads_ok, 3)
                dve.wait_ge(g_ps, g + 1)
                dve.max(t8[:, g], G[:, ER:ER + EXPERTS]).then_inc(t8_ok, 1)
                dve.tensor_copy(lg[:, g, 0:EXPERTS], G[:, ER:ER + EXPERTS]).then_inc(lg_ok, 1)

            def two_greatest(u):
                g = u - TILES
                dve.wait_ge(t8_ok, g + 1)
                dve.wait_ge(lg_ok, g + 1)
                dve.tensor_scalar(nmax[:, g], t8[:, g, 0:1], -1.0, None, ALU.mult).then_inc(nmax_ok, 1)
                dve.tensor_copy(rep[:, g, 0:2], t8[:, g, 0:2]).then_inc(rep_ok, 1)

            def mark(u):
                g = u - TILES
                dve.wait_ge(rep_ok, g + 1)
                dve.match_replace(out=zap[:, g], in_to_replace=rep[:, g], in_values=lg[:, g],
                                  imm_value=TAKEN).then_inc(zap_ok, 1)

            def choose(u):
                g = u - TILES
                dve.wait_ge(zap_ok, g + 1)
                dve.tensor_tensor(chosen[:, g], zap[:, g, 0:EXPERTS], lg[:, g, 0:EXPERTS],
                                  ALU.not_equal).then_inc(chosen_ok, 1)

            def gate_sums(u):
                g = u - TILES
                dve.wait_ge(ge_ok, g + 1)
                dve.reciprocal(grec[:, g], gsum[:, g]).then_inc(grec_ok, 1)

            def weigh(u):
                g = u - TILES
                dve.wait_ge(grec_ok, g + 1)
                dve.wait_ge(chosen_ok, g + 1)
                dve.scalar_tensor_tensor(out=comb[:, g], in0=ge[:, g], scalar=grec[:, g], in1=chosen[:, g],
                                         op0=ALU.mult, op1=ALU.mult).then_inc(comb_ok, 1)

            def weighted(u):
                g = u - TILES
                dve.wait_ge(comb_ok, g + 1)
                dve.tensor_tensor(hw[:, g], G[:, 0:ER].rearrange("p (e r) -> p e r", e=EXPERTS),
                                  comb[:, g].unsqueeze(2).to_broadcast([P, EXPERTS, RANK]),
                                  ALU.mult).then_inc(hw_ok, 1)

            dve.memset(idle[:], 0.0).then_inc(warm_ok, 1)
            dve.memset(hT[ONE:ONE + 1, :, 1, :], 1.0).then_inc(ones_ok, 1)
            dve.memset(cxT[ONE:ONE + 1, :, 1, :], 1.0).then_inc(ones_ok, 1)
            dve.memset(lg[:], NEG).then_inc(pads_ok, 1)
            dve.memset(rep[:], NEG).then_inc(pads_ok, 1)
            dve.memset(zap[:], NEG).then_inc(pads_ok, 1)
            dve.wait_ge(posb_in, 16)
            dve.tensor_tensor(pos[:], posb[:, 0], posb[:, 1], ALU.add).then_inc(pos_ok, 1)
            embedded(0)
            dve.wait_ge(hmask_ok, 2)
            dve.tensor_reduce(first[:, 0:1], head_mask[:, 0:HA:2], AX_X, ALU.add).then_inc(half_ok, 1)
            dve.tensor_reduce(second[:, 0:1], head_mask[:, 1:HA:2], AX_X, ALU.add).then_inc(half_ok, 1)
            dve.wait_ge(half_ok, 2)
            dve.tensor_scalar(first[:, 1:2], first[:, 0:1], ATT_SCALE, None, ALU.mult).then_inc(half_ok, 1)
            dve.tensor_scalar(second[:, 1:2], second[:, 0:1], ATT_SCALE, None, ALU.mult).then_inc(half_ok, 1)
            embedded(1)
            for t in range(UNITS - 1):
                gated = TILES <= t + 1 < UNITS
                spread_keys(t)
                if t + 2 < TILES:
                    embedded(t + 2)
                if t >= 2:
                    residual(t - 2)
                    moments(t - 2)
                if gated:
                    greatest(t + 1)
                    two_greatest(t + 1)
                if t >= 2:
                    mean_variance(t - 2)
                if gated:
                    mark(t + 1)
                    choose(t + 1)
                    gate_sums(t + 1)
                    weigh(t + 1)
                    weighted(t + 1)
                if t >= 1:
                    denominators(t - 1)
                    context(t - 1)
                if t >= 2:
                    normed(t - 2)
                scores(t)
                probs(t)
            u = UNITS - 1
            spread_keys(u)
            low_scores(u)
            scores(u)
            residual(u - 2)
            denominators(u - 1)
            context(u - 1)
            probs(u)
            moments(u - 2)
            mean_variance(u - 2)
            denominators(u)
            context(u)
            normed(u - 2)
            residual(u - 1)
            moments(u - 1)
            mean_variance(u - 1)
            normed(u - 1)
            residual(u)
            moments(u)
            mean_variance(u)
            normed(u)

        @block.tensor
        def _(pe):
            def embed(g):
                pe.wait_ge(x_in[g], 16)
                if g == 0:
                    pe.wait_ge(wtok_in, 16)
                if g >= 2:
                    pe.wait_ge(emb_ok, g)
                for c in range(FC):
                    if g == 0 and c == FC // 2:
                        pe.wait_ge(x_in0b, 16)
                        pe.wait_ge(wtok_in0b, 16)
                    last = pe.matmul(embedding_bank(g)[:, 0:D], xT[:, g, c, :], wtok[:, c, :], start=(c == 0), stop=(c == FC - 1))
                last.then_inc(emb_ps, 1)

            def turn_h(u):
                pe.wait_ge(ident_ok, 1)
                if u < TILES:
                    pe.wait_ge(emb_ok, u + 1)
                else:
                    pe.wait_ge(norm_ok, u - TILES + 1)
                if u >= 2:
                    pe.wait_ge(hT_ok, u)
                if u >= 4:
                    pe.wait_ge(cT_ok, u - 3)
                for c in range(2):
                    last = pe.transpose(turning_bank(u)[0:HALF, HC0 + c * P:HC0 + (c + 1) * P], h[:, u, c * HALF:(c + 1) * HALF], ident[:])
                last.then_inc(hT_ps, 1)

            def gate(u):
                g = u - TILES
                pe.wait_ge(hT_ok, u + 1)
                if g == 0:
                    pe.wait_ge(gw_in, 16)
                else:
                    pe.wait_ge(gT_ok, g)
                for c, rows in enumerate((HALF, ONE + 1)):
                    last = pe.matmul(G[:, 0:ER + EXPERTS], hT[0:rows, u, c, :], gw[0:rows, c, :],
                                     start=(c == 0), stop=(c == 1))
                last.then_inc(g_ps, 1)

            def turn_gated(u):
                g = u - TILES
                pe.wait_ge(hw_ok, g + 1)
                pe.transpose(G[:, 0:P], hw[:, g].rearrange("p e r -> p (e r)"), ident[:])
                pe.transpose(G[0:EXPERTS, P:2 * P], comb[:, g], ident[:]).then_inc(gT_ps, 1)

            def projection(u):
                if u < TILES:
                    return [(w1[0:HALF, 0], hT[0:HALF, u, 0, :]), (w1[0:ONE + 1, 1], hT[0:ONE + 1, u, 1, :])]
                return [(w2[0:ONE + 1, 1], hT[0:ONE + 1, u, 1, :]),
                        (w2[0:HALF + EXPERTS, 0], hT[0:HALF + EXPERTS, u, 0, :]),
                        (lb[:], hwT[:, u - TILES, :])]

            def queries_keys(u):
                pe.wait_ge(hT_ok, u + 1)
                if u == 0:
                    pe.wait_ge(ones_ok, 2)
                    pe.wait_ge(w1_in, 16)
                if u == TILES:
                    pe.wait_ge(w2_in, 16)
                    pe.wait_ge(lb_in, 16)
                if u >= 2:
                    pe.wait_ge(cx_ok, u - 1)
                parts = projection(u)

                def part(out, j, i):
                    w, a = parts[i]
                    return pe.matmul(out, w[:, j * P:(j + 1) * P], a, start=(i == 0), stop=(i == len(parts) - 1))

                part(CX[:, K1C:K1C + P], 1, 0)
                if u >= 1:
                    pe.wait_ge(q_ok, u)
                part(QK[:, 0:P], 0, 0)
                if u >= TILES:
                    pe.wait_ge(gT_ok, u - TILES + 1)
                for i in range(1, len(parts)):
                    last = part(CX[:, K1C:K1C + P], 1, i)
                last.then_inc(k1_ps, 1)
                for i in range(1, len(parts)):
                    part(QK[:, 0:P], 0, i)
                for i in range(len(parts)):
                    last = part(QK[:, P:2 * P], 2, i)
                last.then_inc(qk_ps, 1)

            def values(u):
                if u >= 1:
                    pe.wait_ge(v_ok, u)
                else:
                    pe.wait_ge(emb_ok, 2)
                parts = projection(u)
                for i, (w, a) in enumerate(parts):
                    last = pe.matmul(V[:, 0:D], a, w[:, VC:VC + D], start=(i == 0), stop=(i == len(parts) - 1))
                last.then_inc(v_ps, 1)

            def scores(u):
                pe.wait_ge(q_ok, u + 1)
                pe.wait_ge(kxa_ok, u + 1)
                if u >= 1:
                    pe.wait_ge(sc_ok, u)
                for m in range(PAIRS):
                    r = slice(32 * m, 32 * m + 32)
                    pe.matmul(S[r, 0:HA * PAIR], q1[:, u, r], kxa[:, u % 2, :, r], start=True, stop=True)
                pe.wait_ge(kxb_ok, u + 1)
                for m in range(PAIRS):
                    r = slice(32 * m, 32 * m + 32)
                    last = pe.matmul(S[r, HA * PAIR:HEADS * PAIR], q2[:, u, r], kxb[:, u % 2, :, r],
                                     start=True, stop=True)
                last.then_inc(s_ps, 1)

            def turn_probs(u):
                pe.wait_ge(pa_ok, u + 1)
                pe.wait_ge(pb_ok, u + 1)
                if u >= 1:
                    pe.wait_ge(pT_ok, u)
                rows = prob[:, u].rearrange("p h i k -> p (h i k)")
                for c in range(HC):
                    last = pe.transpose(PT[:, c * P:(c + 1) * P], rows[:, c * P:(c + 1) * P], ident[:])
                last.then_inc(pT_ps, 1)

            def context(u):
                pe.wait_ge(pT_ok, u + 1)
                pe.wait_ge(v_ok, u + 1)
                pe.wait_ge(kxa_ok, min(u + 2, UNITS))
                for c in range(HC):
                    for m in range(PAIRS):
                        r = slice(32 * m, 32 * m + 32)
                        last = pe.matmul(CX[r, c * HQ * (HD + 1):(c + 1) * HQ * (HD + 1)], probT[:, u, c, r],
                                         vx[:, u % 2, m, c].rearrange("p a d -> p (a d)"), start=True, stop=True)
                last.then_inc(cx_ps, 1)

            def turn_ctx(u):
                pe.wait_ge(cx_ok, u + 1)
                if u >= 1:
                    pe.wait_ge(cT_ok, u)
                pe.wait_ge(hT_ok, min(u + 3, UNITS))
                for c in range(2):
                    last = pe.transpose(T[0:HALF, c * P:(c + 1) * P], cx[:, u, c * HALF:(c + 1) * HALF], ident[:])
                last.then_inc(cT_ps, 1)

            def output(u):
                w = w1 if u < TILES else w2
                pe.wait_ge(cT_ok, u + 1)
                if u == 0:
                    pe.wait_ge(emb_ok, TILES)
                else:
                    pe.wait_ge(y_ok, u)
                for c, rows in enumerate((HALF, ONE + 1)):
                    last = pe.matmul(Y[:, 0:D], cxT[0:rows, u, c, :], w[0:rows, c, OC:OC + D],
                                     start=(c == 0), stop=(c == 1))
                last.then_inc(y_ps, 1)

            pe.wait_ge(warm_ok, 1)
            for _ in range(WARM):
                pe.matmul(S[:, 0:512], idle[:, 0:P], idle[:], start=True, stop=True)
            stages = {"embed": embed, "turn_h": turn_h, "gate": gate, "turn_gated": turn_gated,
                      "queries_keys": queries_keys, "values": values, "scores": scores, "turn_probs": turn_probs, "context": context,
                      "turn_ctx": turn_ctx, "output": output}
            for stage, u in [("embed", 0), ("embed", 1), ("turn_h", 0), ("turn_h", 1)]:
                stages[stage](u)
            for t in range(UNITS - 1):
                for stage, u in stages_of(t):
                    stages[stage](u)
            for stage, u in DRAIN:
                stages[stage](u)


def kernel(**inputs):
    import numpy as np
    import concourse.bacc as bacc
    from concourse.bass_utils import run_bass_kernel_spmd

    a = {k: np.asarray(v) for k, v in inputs.items()}
    side = SIDE // PATCH

    x = a["x"].reshape(IMAGES, side, PATCH, side, PATCH, CH).transpose(2, 4, 5, 0, 1, 3)
    xT = x.reshape(FC, P, TILES, P).transpose(2, 1, 0, 3)
    wtok = a["L0_tok_W"].reshape(FC, P, D).transpose(1, 0, 2)
    posb = np.stack([np.tile(a["L0_tok_pos_emb"], (P // NTOK, 1)), np.broadcast_to(a["L0_tok_b"], (P, D))], 1)

    def columns(q, k, v, o):
        return np.concatenate([q[:P], k[:P], q[P:], k[P:], v, o], 0)

    def chunks(w, bias, rows):
        out = np.zeros((rows, 2, w.shape[0]), w.dtype)
        out[:HALF] = w.T.reshape(2, HALF, w.shape[0]).transpose(1, 0, 2)
        out[ONE, 1] = bias
        return out

    w1 = chunks(columns(*(a[f"L0_attn_W{n}"] for n in "qkvo")),
                columns(*(a[f"L0_attn_b{n}"] for n in "qkvo")), ONE + 1)
    wqkv, bqkv = a["L0_ffn_Wqkv"].reshape(3, D, D), a["L0_ffn_bqkv"].reshape(3, D)
    w2 = chunks(columns(*wqkv, a["L0_ffn_Wproj"]), columns(*bqkv, a["L0_ffn_bproj"]), HALF + EXPERTS)
    bb = a["L0_ffn_bb"].T.reshape(3, D, EXPERTS)
    w2[HALF:, 0, :OC] = np.concatenate([bb[0][:P], bb[1][:P], bb[0][P:], bb[1][P:], bb[2]], 0).T
    bm = a["L0_ffn_Bm"].transpose(1, 0, 2).reshape(3, D, ER)
    lb = np.concatenate([bm[0][:P], bm[1][:P], bm[0][P:], bm[1][P:], bm[2]], 0).T
    gw = chunks(np.concatenate([a["L0_ffn_A"].reshape(ER, D), a["L0_ffn_Wg"]], 0),
                np.concatenate([a["L0_ffn_ba"].reshape(ER), a["L0_ffn_bg"]], 0), ONE + 1)

    nc = bacc.Bacc("TRN2", target_bir_lowering=False, num_devices=1)
    arrays, args = {}, []
    for name, v in (("xT", xT), ("wtok", wtok), ("posb", posb), ("w1", w1), ("w2", w2), ("gw", gw), ("lb", lb)):
        v = np.ascontiguousarray(v)
        arrays[f"in_{name}"] = v
        args.append(nc.dram_tensor(f"in_{name}", v.shape, mybir.dt.from_np(v.dtype), kind="ExternalInput").ap())
    args.append(nc.dram_tensor("out_0", (TOKENS, D), F32, kind="ExternalOutput").ap())
    tower(nc, *args)
    r = run_bass_kernel_spmd(nc, [arrays], core_ids=[0])
    return r.results[0]["out_0"].reshape(IMAGES, NTOK, D)
```

```python
from contextlib import ExitStack

import concourse.bass as bass
from concourse import mybir

F32 = mybir.dt.float32
ALU = mybir.AluOpType
ACT = mybir.ActivationFunctionType
AX_X = mybir.AxisListType.X

P = 128
IMAGES, SIDE, PATCH, CH = 32, 64, 16, 3
NTOK = (SIDE // PATCH) ** 2
D = 192
HEADS = 12
HD = D // HEADS
TOKENS = IMAGES * NTOK
TILES = TOKENS // P
UNITS = 2 * TILES
PIX = PATCH * PATCH * CH
FC = PIX // P
HALF = D // 2
ONE = HALF
PAIR = 2 * NTOK
PAIRS = P // PAIR
HA = P // HD
HB = HEADS - HA
DB = D - P
EXPERTS, RANK = 8, 16
ER = EXPERTS * RANK
LORA_SCALE = 2.0
ATT_SCALE = HD ** -0.5
EPS = 1e-5
HQ = P // PAIR
HC = HEADS // HQ
HTC = 2 * P
K1C = 2 * P
PIECES = 3
WARM = 27
FAR = 1.0e4
NEG = -3.0e38
TAKEN = -2.0e38
VC, OC = 3 * P, 3 * P + D
WC = OC + D


def stages_of(t):
    found = (("queries_keys", t), ("embed", t + 2), ("output", t - 2), ("gate", t + 1), ("turn_probs", t - 1),
             ("values", t), ("context", t - 1), ("scores", t), ("turn_gated", t + 1), ("turn_ctx", t - 1),
             ("turn_h", t + 2))
    if t == 0:
        return [("queries_keys", 0), ("turn_h", 2), ("values", 0), ("scores", 0)]
    first = {"gate": TILES, "turn_gated": TILES}
    last = {"embed": TILES}
    return [(stage, u) for stage, u in found if first.get(stage, 0) <= u < last.get(stage, UNITS)]


DRAIN = [("queries_keys", UNITS - 1), ("values", UNITS - 1), ("scores", UNITS - 1), ("output", UNITS - 3),
         ("turn_probs", UNITS - 2), ("idle", 12), ("context", UNITS - 2), ("turn_probs", UNITS - 1),
         ("turn_ctx", UNITS - 2), ("idle", 8), ("context", UNITS - 1), ("output", UNITS - 2),
         ("turn_ctx", UNITS - 1), ("idle", 11), ("output", UNITS - 1)]


def tower(nc, xT_d, wtok_d, posb_d, w1_d, w2_d, gw_d, lb_d, out_d):
    with ExitStack() as ctx:
        def sb(name, shape):
            return ctx.enter_context(nc.sbuf_tensor(name, shape, F32))

        def bank(name):
            return ctx.enter_context(nc.psum_tensor(name, [P, 512], F32))

        def sem(name):
            return ctx.enter_context(nc.semaphore(name))

        xT = sb("xT", [P, TILES, FC, P])
        wtok = sb("wtok", [P, FC, D])
        posb = sb("posb", [P, 2, D])
        pos = sb("pos", [P, D])
        w1 = sb("w1", [ONE + 1, 2, WC])
        w2 = sb("w2", [HALF + EXPERTS, 2, WC])
        gw = sb("gw", [ONE + 1, 2, ER + EXPERTS])
        lb = sb("lb", [P, 3 * P + D])
        idle = ctx.enter_context(nc.sbuf_tensor("idle", [P, P], mybir.dt.bfloat16))
        ident = sb("ident", [P, P])
        head_mask = sb("head_mask", [P, HA])
        first = sb("first", [P, 2])
        second = sb("second", [P, 2])
        off_first = sb("off_first", [P, 1])
        off_second = sb("off_second", [P, 1])
        minus_half = sb("minus_half", [P, 1])
        h = sb("h", [P, UNITS + TILES, D])
        hT = sb("hT", [HALF + EXPERTS, UNITS, 2, P])
        q1 = sb("q1", [P, UNITS, P])
        q2 = sb("q2", [DB, UNITS, P])
        k2 = sb("k2", [DB, UNITS, P])
        kxa = sb("kxa", [P, 2, HA, P])
        kxb = sb("kxb", [DB, 2, HB, P])
        vx = sb("vx", [P, 2, PAIRS, HC, HQ, HD + 1])
        lo = sb("lo", [P, UNITS, HEADS, NTOK])
        sc = sb("sc", [P, UNITS, HEADS, NTOK])
        top = sb("top", [P, UNITS, HEADS])
        rden = sb("rden", [P, UNITS, HEADS])
        prob = sb("prob", [P, UNITS, HEADS, 2, NTOK])
        probT = sb("probT", [P, UNITS, HC, P])
        cx = sb("cx", [P, UNITS, D])
        cxT = sb("cxT", [ONE + 1, UNITS, 2, P])
        y = sb("y", [P, UNITS, D])
        st = sb("st", [P, UNITS, 6])
        mv = sb("mv", [P, UNITS, 2])
        veps = sb("veps", [P, UNITS, 1])
        rstd = sb("rstd", [P, UNITS, 1])
        lg = sb("lg", [P, TILES, 2 * EXPERTS])
        t8 = sb("t8", [P, TILES, 8])
        rep = sb("rep", [P, TILES, 8])
        zap = sb("zap", [P, TILES, 2 * EXPERTS])
        chosen = sb("chosen", [P, TILES, EXPERTS])
        nmax = sb("nmax", [P, TILES, 1])
        ge = sb("ge", [P, TILES, EXPERTS])
        gsum = sb("gsum", [P, TILES, 1])
        grec = sb("grec", [P, TILES, 1])
        comb = sb("comb", [P, TILES, EXPERTS])
        hw = sb("hw", [P, TILES, EXPERTS, RANK])
        hwT = sb("hwT", [P, TILES, P])

        QK, V, S, PT, CX, T, Y, G = [bank("ps_" + n) for n in ("qk", "v", "s", "pt", "cx", "t", "y", "g")]

        x_in = {g: sem(f"x_in{g}") for g in range(1, TILES)}
        x0_in = [sem(f"x0_in{i}") for i in range(PIECES)]
        wtok_in = [sem(f"wtok_in{i}") for i in range(PIECES)]
        posb_in, w1_in, w2_in, gw_in, lb_in = [
            sem(n) for n in ("posb_in", "w1_in", "w2_in", "gw_in", "lb_in")]
        zero_id, ident_ok, hmask_ok, ones_ok, zero_v, pads_ok, pos_ok, half_ok = [
            sem(n) for n in ("zero_id", "ident_ok", "hmask_ok", "ones_ok", "zero_v", "pads_ok", "pos_ok", "half_ok")]
        emb_ps, hT_ps, k1_ps, qk_ps, v_ps, s_ps, pT_ps, cx_ps, cT_ps, y_ps, g_ps, gT_ps = [
            sem(n) for n in ("emb_ps", "hT_ps", "k1_ps", "qk_ps", "v_ps", "s_ps", "pT_ps", "cx_ps", "cT_ps", "y_ps",
                             "g_ps", "gT_ps")]
        hT_ok, k2_ok, q_ok, v_ok, lo_ok, p_ok, pT_ok, cT_ok, ge_ok, gT_ok = [
            sem(n) for n in ("hT_ok", "k2_ok", "q_ok", "v_ok", "lo_ok", "p_ok", "pT_ok", "cT_ok",
                             "ge_ok", "gT_ok")]
        emb_ok, kxa_ok, sc_ok, top_ok, sub_ok, rden_ok, cx_ok, y_ok, st_ok, mv_ok, norm_ok = [
            sem(n) for n in ("emb_ok", "kxa_ok", "sc_ok", "top_ok", "sub_ok",
                             "rden_ok", "cx_ok", "y_ok", "st_ok", "mv_ok", "norm_ok")]
        lg_ok, t8_ok, nmax_ok, rep_ok, zap_ok, chosen_ok, grec_ok, comb_ok, hw_ok = [
            sem(n) for n in ("lg_ok", "t8_ok", "nmax_ok", "rep_ok", "zap_ok", "chosen_ok", "grec_ok",
                             "comb_ok", "hw_ok")]
        kxb_ok, veps_ok, rstd_ok, power_ok = [
            sem(n) for n in ("kxb_ok", "veps_ok", "rstd_ok", "power_ok")]
        warm_ok = sem("warm_ok")
        out_done = sem("out_done")

        def turning_bank(u):
            return G if u == 1 else T

        def embedding_bank(g):
            return V if g == 1 else Y

        def v_part(m, a):
            return V[32 * m:32 * m + 32, 0:D].rearrange("p (c a d) -> p c a d", c=HC, a=HQ)[:, :, a, :]

        def score_part(i):
            return S[:, 0:HEADS * PAIR].rearrange("p (h i k) -> p h i k", h=HEADS, i=2)[:, :, i, :]

        block = ctx.enter_context(nc.Block())

        @block.sync
        def _(sp):
            for i in range(PIECES):
                part = slice(i * FC // PIECES, (i + 1) * FC // PIECES)
                sp.dma_start(xT[:, 0, part], xT_d[0, :, part]).then_inc(x0_in[i], 16)
            sp.dma_start(xT[:, 1], xT_d[1]).then_inc(x_in[1], 16)
            sp.dma_start(xT[:, 2], xT_d[2]).then_inc(x_in[2], 16)
            sp.dma_start(w1[:], w1_d).then_inc(w1_in, 16)
            sp.dma_start(xT[:, 3], xT_d[3]).then_inc(x_in[3], 16)
            sp.dma_start(w2[:], w2_d).then_inc(w2_in, 16)
            for g in range(TILES):
                sp.wait_ge(norm_ok, TILES + g + 1)
                sp.dma_start(out_d[g * P:(g + 1) * P, :], h[:, UNITS + g]).then_inc(out_done, 16)
            sp.wait_ge(out_done, 16 * TILES)

        @block.gpsimd
        def _(pool):
            pool.memset(ident[:], 0.0).then_inc(zero_id, 1)
            pool.memset(head_mask[:], 1.0).then_inc(zero_id, 1)
            pool.wait_ge(zero_id, 1)
            pool.affine_select(out=ident[:], in_=ident[:], compare_op=ALU.not_equal, fill=1.0, base=0,
                               pattern=[[-1, P]], channel_multiplier=1).then_inc(ident_ok, 1)
            pool.wait_ge(zero_id, 2)
            pool.affine_select(out=head_mask[:], in_=head_mask[:], compare_op=ALU.is_ge, fill=0.0, base=0,
                               pattern=[[-HD, HA]], channel_multiplier=1).then_inc(hmask_ok, 1)
            pool.wait_ge(hmask_ok, 1)
            pool.affine_select(out=head_mask[:], in_=head_mask[:], compare_op=ALU.is_ge, fill=0.0, base=HD - 1,
                               pattern=[[HD, HA]], channel_multiplier=-1).then_inc(hmask_ok, 1)
            pool.memset(vx[:], 0.0).then_inc(zero_v, 1)
            pool.wait_ge(zero_v, 1)
            for a in range(HQ):
                pool.memset(vx[32 * a:32 * a + 32, :, :, :, a, HD:HD + 1].rearrange("p b m c o -> p (b m c) o"), 1.0)\
                    .then_inc(zero_v, 1)
            pool.wait_ge(zero_v, 1 + HQ)
            pool.memset(minus_half[:], -0.5).then_inc(power_ok, 1)
            pool.wait_ge(hmask_ok, 2)
            pool.wait_ge(power_ok, 1)

            def spread_keys(u):
                pool.wait_ge(k2_ok, u + 1)
                if u >= 2:
                    pool.wait_ge(s_ps, u - 1)
                pool.tensor_tensor(kxb[:, u % 2], k2[:, u].unsqueeze(1).to_broadcast([DB, HB, P]),
                                   head_mask[0:DB, 0:HB].unsqueeze(2).to_broadcast([DB, HB, P]),
                                   ALU.mult).then_inc(kxb_ok, 1)

            def deviation(u):
                pool.wait_ge(mv_ok, u + 1)
                pool.tensor_scalar(veps[:, u], mv[:, u, 1:2], EPS, None, ALU.add).then_inc(veps_ok, 1)
                pool.wait_ge(veps_ok, u + 1)
                pool.tensor_tensor(rstd[:, u], veps[:, u], minus_half[:], ALU.pow).then_inc(rstd_ok, 1)

            for t in range(UNITS + 2):
                if t < UNITS - 1:
                    spread_keys(t)
                if t >= 2:
                    deviation(t - 2)

        @block.scalar
        def _(act):
            for i in range(PIECES):
                part = slice(i * FC // PIECES, (i + 1) * FC // PIECES)
                act.dma_start(wtok[:, part], wtok_d[:, part]).then_inc(wtok_in[i], 16)
            act.dma_start(posb[:], posb_d).then_inc(posb_in, 16)
            act.dma_start(gw[:], gw_d).then_inc(gw_in, 16)
            act.dma_start(lb[:], lb_d).then_inc(lb_in, 16)

            def turned_h(u):
                act.wait_ge(hT_ps, u + 1)
                turned = turning_bank(u)[0:HALF, HTC:HTC + 2 * P]
                act.activation(hT[0:HALF, u], turned.rearrange("p (c t) -> p c t", c=2),
                               ACT.Copy).then_inc(hT_ok, 1)

            def queries_keys(u):
                act.wait_ge(qk_ps, u + 1)
                act.activation(k2[:, u], QK[DB:P, P:2 * P], ACT.Copy).then_inc(k2_ok, 1)
                act.activation(q1[:, u], QK[:, 0:P], ACT.Copy)
                act.activation(q2[:, u], QK[0:DB, P:2 * P], ACT.Copy).then_inc(q_ok, 1)

            def values(u):
                act.wait_ge(v_ps, u + 1)
                act.wait_ge(zero_v, 1 + HQ)
                if u >= 2:
                    act.wait_ge(cx_ps, u - 1)
                for m in range(PAIRS):
                    for a in range(HQ):
                        last = act.activation(vx[32 * a:32 * a + 32, u % 2, m, :, a, 0:HD], v_part(m, a), ACT.Copy)
                last.then_inc(v_ok, 1)

            def low_scores(u):
                act.wait_ge(s_ps, u + 1)
                act.wait_ge(half_ok, 6)
                act.activation(lo[:, u], score_part(0), ACT.Copy, scale=first[:, 1:2]).then_inc(lo_ok, 1)

            def exps(u):
                act.wait_ge(sub_ok, u + 1)
                for image, off in enumerate((off_first, off_second)):
                    last = act.activation(prob[:, u, :, image, :], sc[:, u], ACT.Exp, bias=off[:])
                last.then_inc(p_ok, 1)

            def turned_probs(u):
                act.wait_ge(pT_ps, u + 1)
                act.activation(probT[:, u], PT[:, 0:HC * P].rearrange("p (c t) -> p c t", c=HC),
                               ACT.Copy).then_inc(pT_ok, 1)

            def turned_ctx(u):
                act.wait_ge(cT_ps, u + 1)
                if u + 3 < UNITS:
                    act.wait_ge(hT_ps, u + 4)
                act.activation(cxT[0:HALF, u], T[0:HALF, 0:2 * P].rearrange("p (c t) -> p c t", c=2),
                               ACT.Copy).then_inc(cT_ok, 1)

            def gate_exps(u):
                g = u - TILES
                act.wait_ge(nmax_ok, g + 1)
                act.activation(ge[:, g], lg[:, g, 0:EXPERTS], ACT.Exp, bias=nmax[:, g],
                               accum_out=gsum[:, g]).then_inc(ge_ok, 1)

            def turned_gated(u):
                g = u - TILES
                act.wait_ge(gT_ps, g + 1)
                act.activation(hwT[:, g], G[:, 0:P], ACT.Copy, scale=LORA_SCALE)
                act.activation(hT[HALF:HALF + EXPERTS, u, 0, :], G[0:EXPERTS, P:2 * P], ACT.Copy,
                               scale=LORA_SCALE).then_inc(gT_ok, 1)

            turned_h(0)
            turned_h(1)
            for t in range(UNITS - 1):
                gated = TILES <= t + 1 < UNITS
                queries_keys(t)
                if t >= 1:
                    turned_probs(t - 1)
                if gated:
                    gate_exps(t + 1)
                values(t)
                low_scores(t)
                if gated:
                    turned_gated(t + 1)
                if t >= 1:
                    turned_ctx(t - 1)
                if t + 2 < UNITS:
                    turned_h(t + 2)
                exps(t)
            u = UNITS - 1
            queries_keys(u)
            values(u)
            turned_probs(u - 1)
            exps(u)
            turned_probs(u)
            turned_ctx(u - 1)
            turned_ctx(u)

        @block.vector
        def _(dve):
            def embedded(g):
                dve.wait_ge(pos_ok, 1)
                dve.wait_ge(emb_ps, g + 1)
                dve.tensor_tensor(h[:, g], embedding_bank(g)[:, 0:D], pos[:], ALU.add).then_inc(emb_ok, 1)

            def spread_keys(u):
                dve.wait_ge(k1_ps, u + 1)
                if u >= 2:
                    dve.wait_ge(s_ps, u - 1)
                dve.tensor_tensor(kxa[:, u % 2], CX[:, K1C:K1C + P].unsqueeze(1).to_broadcast([P, HA, P]),
                                  head_mask[:].unsqueeze(2).to_broadcast([P, HA, P]),
                                  ALU.mult).then_inc(kxa_ok, 1)

            def spread_other_keys(u):
                dve.wait_ge(k2_ok, u + 1)
                dve.wait_ge(s_ps, u - 1)
                dve.tensor_tensor(kxb[:, u % 2], k2[:, u].unsqueeze(1).to_broadcast([DB, HB, P]),
                                  head_mask[0:DB, 0:HB].unsqueeze(2).to_broadcast([DB, HB, P]),
                                  ALU.mult).then_inc(kxb_ok, 1)

            def low_scores(u):
                dve.wait_ge(s_ps, u + 1)
                dve.tensor_scalar(lo[:, u], score_part(0), first[:, 1:2], None, ALU.mult).then_inc(lo_ok, 1)

            def scores(u):
                dve.wait_ge(lo_ok, u + 1)
                dve.scalar_tensor_tensor(out=sc[:, u], in0=score_part(1), scalar=second[:, 1:2], in1=lo[:, u],
                                         op0=ALU.mult, op1=ALU.add).then_inc(sc_ok, 1)
                dve.wait_ge(sc_ok, u + 1)
                dve.tensor_reduce(top[:, u], sc[:, u], AX_X, ALU.max).then_inc(top_ok, 1)
                dve.wait_ge(top_ok, u + 1)
                dve.tensor_tensor(sc[:, u], sc[:, u], top[:, u].unsqueeze(2).to_broadcast([P, HEADS, NTOK]),
                                  ALU.subtract).then_inc(sub_ok, 1)

            def ctx_part():
                return CX[:, 0:HEADS * (HD + 1)].rearrange("p (h d) -> p h d", h=HEADS)

            def denominators(u):
                dve.wait_ge(cx_ps, u + 1)
                dve.reciprocal(rden[:, u].unsqueeze(2), ctx_part()[:, :, HD:HD + 1]).then_inc(rden_ok, 1)

            def context(u):
                dve.wait_ge(rden_ok, u + 1)
                dve.tensor_tensor(cx[:, u].rearrange("p (h d) -> p h d", h=HEADS), ctx_part()[:, :, 0:HD],
                                  rden[:, u].unsqueeze(2).to_broadcast([P, HEADS, HD]),
                                  ALU.mult).then_inc(cx_ok, 1)

            def residual(u):
                dve.wait_ge(y_ps, u + 1)
                if u < TILES:
                    dve.wait_ge(emb_ok, u + 1)
                else:
                    dve.wait_ge(norm_ok, u - TILES + 1)
                dve.tensor_tensor(y[:, u], Y[:, 0:D], h[:, u], ALU.add).then_inc(y_ok, 1)

            def moments(u):
                dve.wait_ge(y_ok, u + 1)
                dve.bn_stats(st[:, u], y[:, u]).then_inc(st_ok, 1)

            def mean_variance(u):
                dve.wait_ge(st_ok, u + 1)
                dve.bn_aggr(mv[:, u], st[:, u]).then_inc(mv_ok, 1)

            def normed(u):
                dve.wait_ge(rstd_ok, u + 1)
                dve.tensor_scalar(h[:, u + TILES], y[:, u], mv[:, u, 0:1], rstd[:, u], ALU.subtract,
                                  ALU.mult).then_inc(norm_ok, 1)

            def greatest(u):
                g = u - TILES
                dve.wait_ge(pads_ok, 3)
                dve.wait_ge(g_ps, g + 1)
                dve.max(t8[:, g], G[:, ER:ER + EXPERTS]).then_inc(t8_ok, 1)
                dve.tensor_copy(lg[:, g, 0:EXPERTS], G[:, ER:ER + EXPERTS]).then_inc(lg_ok, 1)

            def two_greatest(u):
                g = u - TILES
                dve.wait_ge(t8_ok, g + 1)
                dve.wait_ge(lg_ok, g + 1)
                dve.tensor_scalar(nmax[:, g], t8[:, g, 0:1], -1.0, None, ALU.mult).then_inc(nmax_ok, 1)
                dve.tensor_copy(rep[:, g, 0:2], t8[:, g, 0:2]).then_inc(rep_ok, 1)

            def mark(u):
                g = u - TILES
                dve.wait_ge(rep_ok, g + 1)
                dve.match_replace(out=zap[:, g], in_to_replace=rep[:, g], in_values=lg[:, g],
                                  imm_value=TAKEN).then_inc(zap_ok, 1)

            def choose(u):
                g = u - TILES
                dve.wait_ge(zap_ok, g + 1)
                dve.tensor_tensor(chosen[:, g], zap[:, g, 0:EXPERTS], lg[:, g, 0:EXPERTS],
                                  ALU.not_equal).then_inc(chosen_ok, 1)

            def gate_sums(u):
                g = u - TILES
                dve.wait_ge(ge_ok, g + 1)
                dve.reciprocal(grec[:, g], gsum[:, g]).then_inc(grec_ok, 1)

            def weigh(u):
                g = u - TILES
                dve.wait_ge(grec_ok, g + 1)
                dve.wait_ge(chosen_ok, g + 1)
                dve.scalar_tensor_tensor(out=comb[:, g], in0=ge[:, g], scalar=grec[:, g], in1=chosen[:, g],
                                         op0=ALU.mult, op1=ALU.mult).then_inc(comb_ok, 1)

            def weighted(u):
                g = u - TILES
                dve.wait_ge(comb_ok, g + 1)
                dve.tensor_tensor(hw[:, g], G[:, 0:ER].rearrange("p (e r) -> p e r", e=EXPERTS),
                                  comb[:, g].unsqueeze(2).to_broadcast([P, EXPERTS, RANK]),
                                  ALU.mult).then_inc(hw_ok, 1)

            dve.memset(idle[:], 0.0).then_inc(warm_ok, 1)
            dve.memset(hT[ONE:ONE + 1, :, 1, :], 1.0).then_inc(ones_ok, 1)
            dve.memset(cxT[ONE:ONE + 1, :, 1, :], 1.0).then_inc(ones_ok, 1)
            dve.memset(lg[:], NEG).then_inc(pads_ok, 1)
            dve.memset(rep[:], NEG).then_inc(pads_ok, 1)
            dve.memset(zap[:], NEG).then_inc(pads_ok, 1)
            dve.wait_ge(posb_in, 16)
            dve.tensor_tensor(pos[:], posb[:, 0], posb[:, 1], ALU.add).then_inc(pos_ok, 1)
            embedded(0)
            dve.wait_ge(hmask_ok, 2)
            dve.tensor_reduce(first[:, 0:1], head_mask[:, 0:HA:2], AX_X, ALU.add).then_inc(half_ok, 1)
            dve.tensor_reduce(second[:, 0:1], head_mask[:, 1:HA:2], AX_X, ALU.add).then_inc(half_ok, 1)
            dve.wait_ge(half_ok, 2)
            dve.tensor_scalar(first[:, 1:2], first[:, 0:1], ATT_SCALE, None, ALU.mult).then_inc(half_ok, 1)
            dve.tensor_scalar(second[:, 1:2], second[:, 0:1], ATT_SCALE, None, ALU.mult).then_inc(half_ok, 1)
            dve.tensor_scalar(off_first[:], first[:, 0:1], -1.0, FAR, ALU.add, ALU.mult).then_inc(half_ok, 1)
            dve.tensor_scalar(off_second[:], second[:, 0:1], -1.0, FAR, ALU.add, ALU.mult).then_inc(half_ok, 1)
            embedded(1)
            embedded(2)
            for t in range(UNITS - 1):
                gated = TILES <= t + 1 < UNITS
                spread_keys(t)
                if t == 1:
                    embedded(3)
                if t >= 2:
                    residual(t - 2)
                if gated:
                    greatest(t + 1)
                if t >= 2:
                    moments(t - 2)
                if gated:
                    two_greatest(t + 1)
                if t >= 2:
                    mean_variance(t - 2)
                if gated:
                    mark(t + 1)
                    choose(t + 1)
                    gate_sums(t + 1)
                    weigh(t + 1)
                    weighted(t + 1)
                if t >= 1:
                    denominators(t - 1)
                    context(t - 1)
                if t >= 2:
                    normed(t - 2)
                scores(t)
            u = UNITS - 1
            spread_keys(u)
            spread_other_keys(u)
            low_scores(u)
            scores(u)
            residual(u - 2)
            denominators(u - 1)
            context(u - 1)
            moments(u - 2)
            mean_variance(u - 2)
            denominators(u)
            context(u)
            normed(u - 2)
            residual(u - 1)
            moments(u - 1)
            mean_variance(u - 1)
            residual(u)
            moments(u)
            mean_variance(u)
            normed(u - 1)
            normed(u)

        @block.tensor
        def _(pe):
            def embed(g):
                if g >= 1:
                    pe.wait_ge(x_in[g], 16)
                if g >= 2:
                    pe.wait_ge(emb_ok, 1 if g == 2 else g)
                for c in range(FC):
                    if g == 0 and c % (FC // PIECES) == 0:
                        pe.wait_ge(x0_in[c * PIECES // FC], 16)
                        pe.wait_ge(wtok_in[c * PIECES // FC], 16)
                    last = pe.matmul(embedding_bank(g)[:, 0:D], xT[:, g, c, :], wtok[:, c, :],
                                     start=(c == 0), stop=(c == FC - 1))
                last.then_inc(emb_ps, 1)

            def turn_h(u):
                pe.wait_ge(ident_ok, 1)
                if u < TILES:
                    pe.wait_ge(emb_ok, u + 1)
                else:
                    pe.wait_ge(norm_ok, u - TILES + 1)
                if u >= 2:
                    pe.wait_ge(hT_ok, u)
                if u >= 4:
                    pe.wait_ge(cT_ok, u - 3)
                for c in range(2):
                    last = pe.transpose(turning_bank(u)[0:HALF, HTC + c * P:HTC + (c + 1) * P],
                                        h[:, u, c * HALF:(c + 1) * HALF], ident[:])
                last.then_inc(hT_ps, 1)

            def gate(u):
                g = u - TILES
                pe.wait_ge(hT_ok, u + 1)
                if g == 0:
                    pe.wait_ge(gw_in, 16)
                else:
                    pe.wait_ge(gT_ok, g)
                for c, rows in enumerate((HALF, ONE + 1)):
                    last = pe.matmul(G[:, 0:ER + EXPERTS], hT[0:rows, u, c, :], gw[0:rows, c, :],
                                     start=(c == 0), stop=(c == 1))
                last.then_inc(g_ps, 1)

            def turn_gated(u):
                g = u - TILES
                pe.wait_ge(hw_ok, g + 1)
                pe.transpose(G[:, 0:P], hw[:, g].rearrange("p e r -> p (e r)"), ident[:])
                pe.transpose(G[0:EXPERTS, P:2 * P], comb[:, g], ident[:]).then_inc(gT_ps, 1)

            def projection(u):
                if u < TILES:
                    return [(w1[0:HALF, 0], hT[0:HALF, u, 0, :]), (w1[0:ONE + 1, 1], hT[0:ONE + 1, u, 1, :])]
                return [(w2[0:ONE + 1, 1], hT[0:ONE + 1, u, 1, :]),
                        (w2[0:HALF + EXPERTS, 0], hT[0:HALF + EXPERTS, u, 0, :]),
                        (lb[:], hwT[:, u - TILES, :])]

            def value_part(u, i):
                if u == 0 and i == 0:
                    pe.wait_ge(emb_ok, 2)
                elif i == 0:
                    pe.wait_ge(v_ok, u)
                parts = projection(u)
                w, a = parts[i]
                return pe.matmul(V[:, 0:D], a, w[:, VC:VC + D], start=(i == 0), stop=(i == len(parts) - 1))

            def queries_keys(u):
                pe.wait_ge(hT_ok, u + 1)
                if u == 0:
                    pe.wait_ge(ones_ok, 2)
                    pe.wait_ge(w1_in, 16)
                if u == TILES:
                    pe.wait_ge(w2_in, 16)
                    pe.wait_ge(lb_in, 16)
                if u >= 2:
                    pe.wait_ge(cx_ok, u - 1)
                parts = projection(u)

                def part(out, j, i):
                    w, a = parts[i]
                    return pe.matmul(out, w[:, j * P:(j + 1) * P], a, start=(i == 0), stop=(i == len(parts) - 1))

                part(CX[:, K1C:K1C + P], 1, 0)
                if u >= 1:
                    pe.wait_ge(q_ok, u)
                part(QK[:, 0:P], 0, 0)
                if u == UNITS - 1:
                    value_part(u, 0)
                if u >= TILES:
                    pe.wait_ge(gT_ok, u - TILES + 1)
                for i in range(1, len(parts)):
                    last = part(CX[:, K1C:K1C + P], 1, i)
                last.then_inc(k1_ps, 1)
                for i in range(1, len(parts)):
                    part(QK[:, 0:P], 0, i)
                for i in range(len(parts)):
                    last = part(QK[:, P:2 * P], 2, i)
                last.then_inc(qk_ps, 1)

            def values(u):
                for i in range(1 if u == UNITS - 1 else 0, len(projection(u))):
                    last = value_part(u, i)
                last.then_inc(v_ps, 1)

            def scores(u):
                pe.wait_ge(q_ok, u + 1)
                pe.wait_ge(kxa_ok, u + 1)
                if u >= 1:
                    pe.wait_ge(sc_ok, u)
                for m in range(PAIRS):
                    r = slice(32 * m, 32 * m + 32)
                    pe.matmul(S[r, 0:HA * PAIR], q1[:, u, r], kxa[:, u % 2, :, r], start=True, stop=True)
                pe.wait_ge(kxb_ok, u + 1)
                for m in range(PAIRS):
                    r = slice(32 * m, 32 * m + 32)
                    last = pe.matmul(S[r, HA * PAIR:HEADS * PAIR], q2[:, u, r], kxb[:, u % 2, :, r],
                                     start=True, stop=True)
                last.then_inc(s_ps, 1)

            def turn_probs(u):
                pe.wait_ge(p_ok, u + 1)
                if u >= 1:
                    pe.wait_ge(pT_ok, u)
                rows = prob[:, u].rearrange("p h i k -> p (h i k)")
                for c in range(HC):
                    last = pe.transpose(PT[:, c * P:(c + 1) * P], rows[:, c * P:(c + 1) * P], ident[:])
                last.then_inc(pT_ps, 1)

            def context(u):
                pe.wait_ge(pT_ok, u + 1)
                pe.wait_ge(v_ok, u + 1)
                pe.wait_ge(kxa_ok, min(u + 2, UNITS))
                for c in range(HC):
                    for m in range(PAIRS):
                        r = slice(32 * m, 32 * m + 32)
                        last = pe.matmul(CX[r, c * HQ * (HD + 1):(c + 1) * HQ * (HD + 1)], probT[:, u, c, r],
                                         vx[:, u % 2, m, c].rearrange("p a d -> p (a d)"), start=True, stop=True)
                last.then_inc(cx_ps, 1)

            def turn_ctx(u):
                pe.wait_ge(cx_ok, u + 1)
                if u >= 1:
                    pe.wait_ge(cT_ok, u)
                pe.wait_ge(hT_ok, min(u + 3, UNITS))
                for c in range(2):
                    last = pe.transpose(T[0:HALF, c * P:(c + 1) * P], cx[:, u, c * HALF:(c + 1) * HALF], ident[:])
                last.then_inc(cT_ps, 1)

            def output(u):
                w = w1 if u < TILES else w2
                pe.wait_ge(cT_ok, u + 1)
                if u == 0:
                    pe.wait_ge(emb_ok, TILES)
                else:
                    pe.wait_ge(y_ok, u)
                for c, rows in enumerate((HALF, ONE + 1)):
                    last = pe.matmul(Y[:, 0:D], cxT[0:rows, u, c, :], w[0:rows, c, OC:OC + D],
                                     start=(c == 0), stop=(c == 1))
                last.then_inc(y_ps, 1)

            def idle_products(n):
                for _ in range(n):
                    pe.matmul(QK[:, 0:P], idle[:], idle[:], start=True, stop=True)

            def idle_at_end(n):
                pe.wait_ge(q_ok, UNITS)
                idle_products(n)

            pe.wait_ge(warm_ok, 1)
            idle_products(WARM)
            stages = {"embed": embed, "turn_h": turn_h, "gate": gate, "turn_gated": turn_gated,
                      "queries_keys": queries_keys, "values": values, "scores": scores,
                      "turn_probs": turn_probs, "context": context,
                      "turn_ctx": turn_ctx, "output": output, "idle": idle_at_end}
            for stage, u in [("embed", 0), ("embed", 1), ("turn_h", 0), ("embed", 2), ("turn_h", 1)]:
                stages[stage](u)
            for t in range(UNITS - 1):
                for stage, u in stages_of(t):
                    stages[stage](u)
            for stage, u in DRAIN:
                stages[stage](u)


def kernel(**inputs):
    import numpy as np
    import concourse.bacc as bacc
    from concourse.bass_utils import run_bass_kernel_spmd

    a = {k: np.asarray(v) for k, v in inputs.items()}
    side = SIDE // PATCH

    x = a["x"].reshape(IMAGES, side, PATCH, side, PATCH, CH).transpose(2, 4, 5, 0, 1, 3)
    xT = x.reshape(FC, P, TILES, P).transpose(2, 1, 0, 3)
    wtok = a["L0_tok_W"].reshape(FC, P, D).transpose(1, 0, 2)
    posb = np.stack([np.tile(a["L0_tok_pos_emb"], (P // NTOK, 1)), np.broadcast_to(a["L0_tok_b"], (P, D))], 1)

    def columns(q, k, v, o):
        return np.concatenate([q[:P], k[:P], q[P:], k[P:], v, o], 0)

    def chunks(w, bias, rows):
        out = np.zeros((rows, 2, w.shape[0]), w.dtype)
        out[:HALF] = w.T.reshape(2, HALF, w.shape[0]).transpose(1, 0, 2)
        out[ONE, 1] = bias
        return out

    w1 = chunks(columns(*(a[f"L0_attn_W{n}"] for n in "qkvo")),
                columns(*(a[f"L0_attn_b{n}"] for n in "qkvo")), ONE + 1)
    wqkv, bqkv = a["L0_ffn_Wqkv"].reshape(3, D, D), a["L0_ffn_bqkv"].reshape(3, D)
    w2 = chunks(columns(*wqkv, a["L0_ffn_Wproj"]), columns(*bqkv, a["L0_ffn_bproj"]), HALF + EXPERTS)
    bb = a["L0_ffn_bb"].T.reshape(3, D, EXPERTS)
    w2[HALF:, 0, :OC] = np.concatenate([bb[0][:P], bb[1][:P], bb[0][P:], bb[1][P:], bb[2]], 0).T
    bm = a["L0_ffn_Bm"].transpose(1, 0, 2).reshape(3, D, ER)
    lb = np.concatenate([bm[0][:P], bm[1][:P], bm[0][P:], bm[1][P:], bm[2]], 0).T
    gw = chunks(np.concatenate([a["L0_ffn_A"].reshape(ER, D), a["L0_ffn_Wg"]], 0),
                np.concatenate([a["L0_ffn_ba"].reshape(ER), a["L0_ffn_bg"]], 0), ONE + 1)

    nc = bacc.Bacc("TRN2", target_bir_lowering=False, num_devices=1)
    arrays, args = {}, []
    for name, v in (("xT", xT), ("wtok", wtok), ("posb", posb), ("w1", w1), ("w2", w2), ("gw", gw), ("lb", lb)):
        v = np.ascontiguousarray(v)
        arrays[f"in_{name}"] = v
        args.append(nc.dram_tensor(f"in_{name}", v.shape, mybir.dt.from_np(v.dtype), kind="ExternalInput").ap())
    args.append(nc.dram_tensor("out_0", (TOKENS, D), F32, kind="ExternalOutput").ap())
    tower(nc, *args)
    r = run_bass_kernel_spmd(nc, [arrays], core_ids=[0])
    return r.results[0]["out_0"].reshape(IMAGES, NTOK, D)
```
